# Optimizing a Trainium2 kernel written in Bass

```python
import numpy as np
import jax
import jax.numpy as jnp

def _softmax(x, axis=-1):
    return jax.nn.softmax(x, axis=axis)

def _gelu(x):
    return jax.nn.gelu(x, approximate=True)

def _silu(x):
    return jax.nn.silu(x)

def _sigmoid(x):
    return jax.nn.sigmoid(x)

def _layernorm(x, axis=-1, eps=1e-05):
    m = jnp.mean(x, axis=axis, keepdims=True)
    v = jnp.var(x, axis=axis, keepdims=True)
    return (x - m) / jnp.sqrt(v + eps)

def _scatter_add(tgt, idx, src, axis=0):
    return tgt.at[idx].add(src)

def _segment_sum(src, seg, n):
    return jax.ops.segment_sum(src, seg, n)
kernel_name = 'mk_decoder_postln_d1_seqx_r8_68f05f'

def setup_inputs(seed: int=0):
    np.random.seed(seed)
    _w = jnp.asarray

    def _rec_inputs():
        import jax
        import jax.numpy as jnp
        _rk = jax.random.key(seed)
        x = -0.000125 + 0.9999 * jax.random.normal(jax.random.fold_in(_rk, 1), (2, 256, 512), jnp.float32)
        _lenS = 256 - jax.random.randint(jax.random.fold_in(_rk, 7), (2,), 0, max(1, 256 // 4) + 1, jnp.int32)
        _lenS2 = 512 - jax.random.randint(jax.random.fold_in(_rk, 8), (2,), 0, max(1, 512 // 4) + 1, jnp.int32)
        _ctx_4096P = jax.random.normal(jax.random.fold_in(_rk, 11), (2, 16, 512), jnp.float32)
        _ctx_4096c = jax.random.dirichlet(jax.random.fold_in(_rk, 511), 0.3 * jnp.ones((16,), jnp.float32), (2, 512))
        _ctx_4096t = jnp.einsum('bsk,bkd->bsd', _ctx_4096c, _ctx_4096P)
        _ctx_4096t = _ctx_4096t * jax.lax.rsqrt(jnp.mean(jnp.square(_ctx_4096t)) + 1e-12) * 0.953939
        ctx_4096 = -5.72187e-05 + 0.999849 * (_ctx_4096t + 0.3 * jax.random.normal(jax.random.fold_in(_rk, 611), (2, 512, 512), jnp.float32))
        return (x, ctx_4096)
    x, ctx_4096 = _rec_inputs()

    def _L0_attn_setup():
        import jax, jax.numpy as jnp
        import numpy as np
        H = 32
        HKV = 8
        D = 512
        HD = D // H
        S = 128
        MASK_OUT = 0.9
        MIN_REMAIN = 128
        THETA = 10000.0

        def rope_tables(seq_len, hd):
            inv_freq = 1.0 / THETA ** (jnp.arange(0, hd, 2, dtype=jnp.float32) / hd)
            t = jnp.arange(seq_len, dtype=jnp.float32)
            freqs = jnp.outer(t, inv_freq)
            emb = jnp.concatenate([freqs, freqs], axis=-1)
            return (jnp.cos(emb), jnp.sin(emb))

        def rotate_half(x):
            x1, x2 = jnp.split(x, 2, axis=-1)
            return jnp.concatenate([-x2, x1], axis=-1)

        def apply_rope(x, cos, sin):
            return x * cos + rotate_half(x) * sin
        key = jax.random.key(seed)
        k0, k1, k2, k3, k4 = jax.random.split(key, 5)
        hidden_states = jax.random.normal(k0, (1, S, D), jnp.float32)
        Wq = jax.random.normal(k1, (D, D), jnp.float32) * 0.02
        Wk = jax.random.normal(k2, (HKV * HD, D), jnp.float32) * 0.02
        Wv = jax.random.normal(k3, (HKV * HD, D), jnp.float32) * 0.02
        Wo = jax.random.normal(k4, (D, D), jnp.float32) * 0.02
        return {'hidden_states': hidden_states, 'Wq': Wq, 'Wk': Wk, 'Wv': Wv, 'Wo': Wo}
    _L0_attn_all = _L0_attn_setup()
    _L0_attn_in = {k: v for k, v in _L0_attn_all.items() if k in ('Wq', 'Wk', 'Wv', 'Wo')}
    del _L0_attn_all

    def _L0_xattn_setup():
        import jax, jax.numpy as jnp
        import numpy as np
        QMIN = 0.0
        QMAX = 255.0

        def fake_quant(x, scale, zp):
            s = scale.reshape(())
            z = zp.reshape(())
            q = jnp.clip(jnp.round(x / s + z), QMIN, QMAX)
            return (q - z) * s
        key = jax.random.key(seed)
        k1, k2 = jax.random.split(key)
        B, M, K, N = (4, 256, 512, 512)
        x1 = jax.random.normal(k1, (B, M, K), dtype=jnp.float32)
        x2 = jax.random.normal(k2, (B, K, N), dtype=jnp.float32)
        x1_scale = jnp.full((1,), 8.0 / 255.0, dtype=jnp.float32)
        x1_zp = jnp.full((1,), 128.0, dtype=jnp.float32)
        x2_scale = jnp.full((1,), 8.0 / 255.0, dtype=jnp.float32)
        x2_zp = jnp.full((1,), 128.0, dtype=jnp.float32)
        return {'x1': x1, 'x2': x2, 'x1_scale': x1_scale, 'x1_zp': x1_zp, 'x2_scale': x2_scale, 'x2_zp': x2_zp}
    _L0_xattn_all = _L0_xattn_setup()
    _L0_xattn_in = {k: v for k, v in _L0_xattn_all.items() if k in ('x1_scale', 'x1_zp', 'x2_scale', 'x2_zp')}
    del _L0_xattn_all

    def _L0_ffn_setup():
        import jax, jax.numpy as jnp
        import numpy as np
        D_MODEL = 512
        D_FF = 1376

        def _dequant_linear(x, w_int, scale):
            return jnp.einsum('bsd,fd->bsf', x, w_int.astype(x.dtype)) * scale
        key = jax.random.key(seed)
        ks = jax.random.split(key, 7)
        x = jax.random.normal(ks[0], (2, 256, D_MODEL), dtype=jnp.float32)
        gate_w = jax.random.randint(ks[1], (D_FF, D_MODEL), -127, 127, dtype=jnp.int32)
        up_w = jax.random.randint(ks[2], (D_FF, D_MODEL), -127, 127, dtype=jnp.int32)
        down_w = jax.random.randint(ks[3], (D_MODEL, D_FF), -127, 127, dtype=jnp.int32)
        gate_s = jax.random.uniform(ks[4], (D_FF,), dtype=jnp.float32) * 0.01 + 0.001
        up_s = jax.random.uniform(ks[5], (D_FF,), dtype=jnp.float32) * 0.01 + 0.001
        down_s = jax.random.uniform(ks[6], (D_MODEL,), dtype=jnp.float32) * 0.01 + 0.001
        return {'x': x, 'gate_w': gate_w, 'gate_s': gate_s, 'up_w': up_w, 'up_s': up_s, 'down_w': down_w, 'down_s': down_s}
    _L0_ffn_all = _L0_ffn_setup()
    _L0_ffn_in = {k: v for k, v in _L0_ffn_all.items() if k in ('gate_w', 'gate_s', 'up_w', 'up_s', 'down_w', 'down_s')}
    del _L0_ffn_all
    return {'x': x, 'ctx_4096': ctx_4096, 'L0_attn_Wq': _L0_attn_in['Wq'], 'L0_attn_Wk': _L0_attn_in['Wk'], 'L0_attn_Wv': _L0_attn_in['Wv'], 'L0_attn_Wo': _L0_attn_in['Wo'], 'L0_xattn_x1_scale': _L0_xattn_in['x1_scale'], 'L0_xattn_x1_zp': _L0_xattn_in['x1_zp'], 'L0_xattn_x2_scale': _L0_xattn_in['x2_scale'], 'L0_xattn_x2_zp': _L0_xattn_in['x2_zp'], 'L0_ffn_gate_w': _L0_ffn_in['gate_w'], 'L0_ffn_gate_s': _L0_ffn_in['gate_s'], 'L0_ffn_up_w': _L0_ffn_in['up_w'], 'L0_ffn_up_s': _L0_ffn_in['up_s'], 'L0_ffn_down_w': _L0_ffn_in['down_w'], 'L0_ffn_down_s': _L0_ffn_in['down_s']}

def reference(x, ctx_4096, L0_attn_Wq, L0_attn_Wk, L0_attn_Wv, L0_attn_Wo, L0_xattn_x1_scale, L0_xattn_x1_zp, L0_xattn_x2_scale, L0_xattn_x2_zp, L0_ffn_gate_w, L0_ffn_gate_s, L0_ffn_up_w, L0_ffn_up_s, L0_ffn_down_w, L0_ffn_down_s):
    import jax
    import jax.numpy as jnp

    def _L0_attn_ref(hidden_states, Wq, Wk, Wv, Wo):
        import jax, jax.numpy as jnp
        import numpy as np
        H = 32
        HKV = 8
        D = 512
        HD = D // H
        S = 128
        MASK_OUT = 0.9
        MIN_REMAIN = 128
        THETA = 10000.0

        def rope_tables(seq_len, hd):
            inv_freq = 1.0 / THETA ** (jnp.arange(0, hd, 2, dtype=jnp.float32) / hd)
            t = jnp.arange(seq_len, dtype=jnp.float32)
            freqs = jnp.outer(t, inv_freq)
            emb = jnp.concatenate([freqs, freqs], axis=-1)
            return (jnp.cos(emb), jnp.sin(emb))

        def rotate_half(x):
            x1, x2 = jnp.split(x, 2, axis=-1)
            return jnp.concatenate([-x2, x1], axis=-1)

        def apply_rope(x, cos, sin):
            return x * cos + rotate_half(x) * sin
        B, Sq, Dm = hidden_states.shape
        dtype = hidden_states.dtype
        neg = jnp.finfo(dtype).min
        q = (hidden_states @ Wq.T).reshape(B, Sq, H, HD).transpose(0, 2, 1, 3)
        k = (hidden_states @ Wk.T).reshape(B, Sq, HKV, HD).transpose(0, 2, 1, 3)
        v = (hidden_states @ Wv.T).reshape(B, Sq, HKV, HD).transpose(0, 2, 1, 3)
        rep = H // HKV
        k = jnp.repeat(k, rep, axis=1)
        v = jnp.repeat(v, rep, axis=1)
        cos, sin = rope_tables(Sq, HD)
        qr = apply_rope(q, cos, sin)
        kr = apply_rope(k, cos, sin)
        draft = jnp.einsum('bhqd,bhkd->bhqk', qr, kr)
        qi = jnp.arange(Sq)
        ki = jnp.arange(Sq)
        causal_future = qi[:, None] < ki[None, :]
        draft = draft + jnp.where(causal_future, neg, jnp.asarray(0.0, dtype))
        num_remain = max(min(Sq, MIN_REMAIN), Sq - int(Sq * MASK_OUT))
        _, draft_indices = jax.lax.top_k(draft, num_remain)
        mask = jnp.full((B, H, Sq, Sq), neg, dtype)
        b_idx = jnp.arange(B)[:, None, None, None]
        h_idx = jnp.arange(H)[None, :, None, None]
        s_idx = jnp.arange(Sq)[None, None, :, None]
        mask = mask.at[b_idx, h_idx, s_idx, draft_indices].set(0.0)
        mask = jnp.where(causal_future[None, None, :, :], neg, mask)
        scores = jnp.einsum('bhqd,bhkd->bhqk', qr, kr) / np.sqrt(HD).astype(np.float32) + mask
        attn = jax.nn.softmax(scores, axis=-1)
        out = jnp.einsum('bhqk,bhkd->bhqd', attn, v)
        out = out.transpose(0, 2, 1, 3).reshape(B, Sq, Dm)
        return out @ Wo.T

    def _L0_xattn_ref(x1, x2, x1_scale, x1_zp, x2_scale, x2_zp):
        import jax, jax.numpy as jnp
        import numpy as np
        QMIN = 0.0
        QMAX = 255.0

        def fake_quant(x, scale, zp):
            s = scale.reshape(())
            z = zp.reshape(())
            q = jnp.clip(jnp.round(x / s + z), QMIN, QMAX)
            return (q - z) * s
        q1 = fake_quant(x1, x1_scale, x1_zp)
        q2 = fake_quant(x2, x2_scale, x2_zp)
        return jnp.matmul(q1, q2)

    def _L0_ffn_ref(x, gate_w, gate_s, up_w, up_s, down_w, down_s):
        import jax, jax.numpy as jnp
        import numpy as np
        D_MODEL = 512
        D_FF = 1376

        def _dequant_linear(x, w_int, scale):
            return jnp.einsum('bsd,fd->bsf', x, w_int.astype(x.dtype)) * scale
        gate = jax.nn.silu(_dequant_linear(x, gate_w, gate_s))
        up = _dequant_linear(x, up_w, up_s)
        h = gate * up
        return _dequant_linear(h, down_w, down_s)
    x = _layernorm(x + _L0_attn_ref(x, L0_attn_Wq, L0_attn_Wk, L0_attn_Wv, L0_attn_Wo), axis=-1)
    x = _layernorm(x + _L0_xattn_ref(x, ctx_4096, L0_xattn_x1_scale, L0_xattn_x1_zp, L0_xattn_x2_scale, L0_xattn_x2_zp), axis=-1)
    x = _layernorm(x + _L0_ffn_ref(x, L0_ffn_gate_w, L0_ffn_gate_s, L0_ffn_up_w, L0_ffn_up_s, L0_ffn_down_w, L0_ffn_down_s), axis=-1)
    return x

_drawn_inputs = setup_inputs


def setup_inputs(seed=0):
    import zlib

    import numpy as np

    out = dict(_drawn_inputs(seed))
    spreads = {}
    factors = {}
    for name, (base, spread) in spreads.items():
        noise = np.random.default_rng([zlib.crc32(name.encode()), seed]).standard_normal(out[name].shape)
        drawn = base * np.exp(spread * noise) if base else spread * noise
        out[name] = jnp.asarray(drawn.astype(out[name].dtype))
    for name, factor in factors.items():
        out[name] = (out[name] * factor).astype(out[name].dtype)
    return out
```

```python
from contextlib import ExitStack
import math

import concourse.bass as bass
from concourse import mybir
import numpy as np

P = 128
B, SEQ, D = 2, 256, 512
H, HKV, HD = 32, 8, 16
REP = H // HKV
DKV = HKV * HD
DFF = 1376
KD = D // P
NF = -(-DFF // P)
QT = SEQ // P
NQK = H + HKV
NSLOT = P // HD
NPART = 3
KEEP = 128
ROUNDS = KEEP // 8
HALVES = 2
HU = H // HALVES
NU = B * HALVES
GU = HU // REP
VC = HD + 1
NR = 3
THETA = 10000.0
SHRINK = 2.0 ** -40
SCALE = 0.25 / SHRINK
MASKED = -0.5
TAKEN = -1.0
COUNTS = 3
SLACK = 7
BOLD = 1.1
SQRT_BITS = 532487669.0
RSQRT_BITS = float(0x5F3759DF)
MAGIC = float(2 ** 23)
QMID = 128.0
QMAX = 255.0
EPS = 1e-5

F32, BF16, I32 = mybir.dt.float32, mybir.dt.bfloat16, mybir.dt.int32
ALU = mybir.AluOpType
ACT = mybir.ActivationFunctionType
AX_X = mybir.AxisListType.X



def schedule():
    out = []

    def scored(u):
        for g in range(GU):
            out.extend([("scores", u, g), ("early_values", u, g)])
        out.extend([("early_norm", u), ("guess", u)])

    for tt in range(QT):
        out.append(("project", tt))
    scored(0)
    out.extend([("context", 0), ("context", 1), ("count", 0, 0)])
    scored(1)
    out.extend([("adjust", 0, 0), ("count", 0, 1), ("project", QT), ("adjust", 0, 1), ("count", 0, 2),
                ("project", QT + 1), ("weights", 0)])
    post = []

    def fill(n):
        for _ in range(min(n, len(post))):
            out.append(post.pop(0))

    for u in range(NU):
        nxt = u + 1 < NU
        if nxt:
            out.append(("count", u + 1, 0))
        out.append(("aim", u))
        for h in range(HU // 2):
            out.append(("eight", u, h))
            if h % 2:
                fill(1)
        if nxt:
            out.extend([("adjust", u + 1, 0), ("count", u + 1, 1)])
        out.append(("late_exp", u))
        for h in range(HU // 2, HU):
            out.append(("eight", u, h))
            if h % 2:
                fill(1)
        out.append(("pick", u))
        if nxt:
            out.extend([("adjust", u + 1, 1), ("count", u + 1, 2)])
        fill(1)
        out.append(("keep", u))
        fill(1)
        for g in range(GU):
            out.append(("late_values", u, g))
        out.append(("late_norm", u))
        if u + 2 < NU:
            scored(u + 2)
        if u % HALVES == HALVES - 1:
            b = u // HALVES
            post = [(name, b) for name in ("out_turn", "out_project", "norm_quantise", "cross_turn", "cross_product",
                                           "norm_turn")]
            post += [("hidden", b, f) for f in range(NF)] + [("finish", b)]
    fill(len(post))
    return out


def decoder_layer(nc, x, xT, ctx, wqkvT, woT, scal, ffw, gus, down_s, rope, consts, out):
    steps_in_order = schedule()

    with ExitStack() as stack:
        def sb(name, shape, dt=F32):
            return stack.enter_context(nc.sbuf_tensor(name, shape, dt))

        def ps(name, shape, dt=F32):
            return stack.enter_context(nc.psum_tensor(name, shape, dt))

        def sem(name):
            return stack.enter_context(nc.semaphore(name))

        x_sb = sb("x_sb", [P, B * QT, D])
        front = sb("front", [P, KD * (B * SEQ + D + 2 * DKV)])
        xT_sb = front[:, 0:KD * B * SEQ].rearrange("p (k t) -> p k t", k=KD)
        wqkv = front[:, KD * B * SEQ:].rearrange("p (k n) -> p k n", k=KD)
        ff = [front[:, i * 3 * D:(i + 1) * 3 * D] for i in range(NR)]
        wo = sb("wo", [P, KD, D])
        ctx_q = sb("ctx_q", [P, B, KD, D], BF16)
        gus_sb = sb("gus_sb", [P, 2, NF])
        gate_half = sb("gate_half", [P, NF])
        both_half = sb("both_half", [P, NF])
        ds = sb("ds", [P, D])
        sc = sb("sc", [P, 4])
        inv = sb("inv", [P, 4])
        zc = sb("zc", [P, 4])
        rope_sb = sb("rope_sb", [P, QT, 2, 2, HD])
        cst = sb("cst", [P, 2 * P + 16])
        identf = cst[:, 0:P]
        z_neg, k_unit = cst[:, 2 * P:2 * P + 1], cst[:, 2 * P + 1:2 * P + 2]
        places = cst[:, 2 * P + 2:2 * P + 10]
        identb = sb("identb", [P, P], BF16)
        causal = sb("causal", [P, P], BF16)
        onesb = sb("onesb", [P, P], BF16)
        onesf = sb("onesf", [P, 1])
        middle = sb("middle", [P, max(NF * SEQ + 2 * SEQ, NQK * (P + NPART * HD) // 2)])
        nat = middle[:, 0:NQK * P // 2].bitcast(BF16).rearrange("p (h s d) -> p h s d", h=NQK, s=NSLOT)
        parts = middle[:, NQK * P // 2:NQK * P // 2 + NQK * NPART * HD // 2].bitcast(BF16).rearrange(
            "p (h s d) -> p h s d", h=NQK, s=NPART)
        hT = middle[:, 0:NF * SEQ].rearrange("p (f t) -> p f t", f=NF)
        g_sb = middle[:, NF * SEQ:NF * SEQ + 2 * SEQ].rearrange("p (a t) -> p a t", a=2)
        rot = sb("rot", [P, NQK, HD])
        rot2 = sb("rot2", [P, NQK, HD])
        qst = sb("qst", [P, NQK, SEQ], BF16)
        vaug = sb("vaug", [P, B, QT, HKV, VC])
        S = sb("S", [P, 2, HU, SEQ])
        E = sb("E", [P, HU, SEQ])
        EL = sb("EL", [P, HU, P])
        Z = sb("Z", [P, 4, SEQ])
        W = sb("W", [P, 3, SEQ])
        m8 = sb("m8", [P, 8])
        plain = sb("plain", [P, 1, SEQ])
        taken = sb("taken", [P, 1, SEQ])
        V = sb("V", [P, HU, 8])
        hot = sb("hot", [P, HU, 8])
        hot2 = sb("hot2", [P, HU, 8])
        st = sb("st", [P, HU, 6])
        smax = sb("smax", [P, QT, HU])
        nmax = sb("nmax", [P, 2, QT, HU])
        tiny = {n: sb(n, [P, 2, HU]) for n in ("nt", "kk", "sg", "sg_old", "size")}
        temp = {n: sb(n, [P, HU]) for n in ("t0", "t1", "t2", "mag", "sigma", "tau", "theta", "vm", "vn", "flag")}
        flag_row = sb("flag_row", [P, 2 * HU], I32)
        flag_sum = sb("flag_sum", [P, 1])
        flag_any = sb("flag_any", [P, 1], I32)
        ptL = sb("ptL", [P, REP, P])
        ptU = sb("ptU", [P, REP, QT, P])
        rsum = sb("rsum", [P, HU])
        A = sb("A", [P, B * QT, D])
        junk = sb("junk", [P, 4, SEQ], BF16)
        xt2 = sb("xt2", [P, KD, SEQ])
        r1 = sb("r1", [P, QT, D])
        x1 = sb("x1", [P, QT, D])
        aq = sb("aq", [P, QT, D], BF16)
        aqT = sb("aqT", [P, KD, SEQ], BF16)
        cadd = sb("cadd", [P, B, D])
        arow = sb("arow", [P, QT])
        st6 = sb("st6", [P, QT, 6])
        mv = sb("mv", [P, QT, 2])
        var = sb("var", [P, QT])
        rstd = sb("rstd", [P, QT])
        sq = sb("sq", [P, QT])

        bS = [ps("bS0", [P, 512]), ps("bS1", [P, 512])]
        bT = [ps("bT0", [P, 512]), ps("bT1", [P, 512])]
        bO = ps("bO", [P, 512])
        bG = [ps("bG0", [P, 512]), ps("bG1", [P, 512])]
        bD = ps("bD", [P, 512])

        names = """scale_ready in_gus in_x in_w in_cst in_ctx in_tok in_wo cst_ready
            dve act qkv_ready qkv_used parts_ready slots_ready heads_ready heads_copied
            late_ready late_used early_ready nmax_ready late_exp early_exp late_prob
            early_turned early_copied early_pv early_norm late_turned late_copied late_pv late_norm
            guess_ready counted adjusted aimed z_made w_made top_made flag_ready flag_summed
            a_turned out_copied out_ready quant_ready cross_turned cross_copied cross_ready
            colsum_ready cadd_ready ctx_ready norm_ready x_turned x_copied
            gate_up_ready gate_done h_ready ff_used down_ready down_used y_ready out_done""".split()
        s = {n: sem(n) for n in names}
        in_ff = [sem(f"in_ff{i}") for i in range(NR)]

        def walk(handlers):
            for step in steps_in_order:
                if step[0] in handlers:
                    handlers[step[0]](*step[1:])

        block = stack.enter_context(nc.Block())

        @block.sync
        def _(sp):
            sp.dma_start(xT_sb, xT.rearrange("(k p) t -> p k t", p=P)).then_inc(s["in_x"], 16)
            sp.dma_start(wqkv, wqkvT.rearrange("(k p) n -> p k n", p=P)).then_inc(s["in_w"], 16)
            sp.dma_start(cst[:], consts).then_inc(s["in_cst"], 16)
            sp.dma_start(rope_sb[:], rope.rearrange("(t p) a r d -> p t a r d", p=P)).then_inc(s["in_cst"], 16)
            sp.dma_start(sc[:], scal[None, :].broadcast_to([P, 4])).then_inc(s["in_cst"], 16)
            sp.dma_start(gus_sb[:], gus).then_inc(s["in_gus"], 16)
            sp.dma_start(E[:].rearrange("p (b k a) n -> p b k (a n)", b=B, k=KD),
                         ctx.rearrange("b (k p) n -> p b k n", p=P)).then_inc(s["in_ctx"], 16)
            sp.dma_start(x_sb[:], x.rearrange("b (t p) d -> p (b t) d", p=P)).then_inc(s["in_tok"], 16)
            sp.dma_start(ds[:], down_s[None, :].broadcast_to([P, D])).then_inc(s["in_tok"], 16)
            sp.dma_start(wo[:], woT.rearrange("(k p) n -> p k n", p=P)).then_inc(s["in_wo"], 16)
            for b in range(B):
                sp.wait_ge(s["y_ready"], QT * (b + 1))
                sp.dma_start(out[b].rearrange("(t p) d -> p t d", p=P), x1[:]).then_inc(s["out_done"], 16)
            sp.wait_ge(s["out_done"], 16 * B)

        NSLOTS = 6

        @block.gpsimd
        def _(pool):
            def load(n):
                pool.dma_start(ff[n % NR], ffw[n % NF]).then_inc(in_ff[n % NR], 16)

            def project(tt):
                pool.wait_ge(s["parts_ready"], tt + 1)
                if tt >= 1:
                    pool.wait_ge(s["heads_ready"], tt * NQK // 8)
                q, k = nat[:, 0:H], nat[:, H:NQK]
                for lo, hi in ((0, 3), (3, 6), (6, 8)):
                    nc.gpsimd.tensor_copy(q[:, :, lo:hi, :], parts[:, 0:H, 0:hi - lo, :]).then_inc(s["slots_ready"], 1)
                for part, lo, hi in ((0, 0, 3), (1, 3, 6), (2, 6, 8)):
                    src = parts[:, H:NQK, part:part + 1, :].broadcast_to([P, HKV, hi - lo, HD])
                    nc.gpsimd.tensor_copy(k[:, :, lo:hi, :], src).then_inc(s["slots_ready"], 1)

            def weights(_):
                pool.wait_ge(s["qkv_ready"], B * QT)
                for n in range(NR):
                    load(n)

            def hidden(b, f):
                n = b * NF + f
                if n >= 1 and n - 1 + NR < B * NF:
                    pool.wait_ge(s["ff_used"], n)
                    load(n - 1 + NR)

            def context(b):
                if b == 0:
                    pool.wait_ge(s["in_ctx"], 16)
                    pool.wait_ge(s["scale_ready"], 1)
                c = E[:, b * HU // 2:(b + 1) * HU // 2, :].rearrange("p (k a) n -> p k (a n)", k=KD)
                base = 4 * b
                nc.gpsimd.tensor_scalar(c, c, inv[:, 2:3], sc[:, 3:4], ALU.mult, ALU.add).then_inc(s["ctx_ready"], 1)
                pool.wait_ge(s["ctx_ready"], base + 1)
                nc.gpsimd.tensor_scalar(c, c, QMAX, 0.0, ALU.min, ALU.max).then_inc(s["ctx_ready"], 1)
                pool.wait_ge(s["ctx_ready"], base + 2)
                nc.gpsimd.tensor_scalar(c, c, MAGIC, 1.0, ALU.add, ALU.mult).then_inc(s["ctx_ready"], 1)
                pool.wait_ge(s["ctx_ready"], base + 3)
                nc.gpsimd.tensor_scalar(ctx_q[:, b], c, -(MAGIC + QMID), 1.0, ALU.add,
                                        ALU.mult).then_inc(s["ctx_ready"], 1)

            def eight(u, h):
                n = u * HU + h
                if h == 0:
                    pool.wait_ge(s["aimed"], u + 1)
                if n >= 4:
                    pool.wait_ge(s["w_made"], n - 3)
                nc.gpsimd.tensor_scalar(Z[:, h % 4, :], S[:, u % 2, h, :], temp["sigma"][:, h:h + 1], 1.0,
                                        ALU.mult, ALU.mult).then_inc(s["z_made"], 1)

            walk({"project": project, "weights": weights, "hidden": hidden, "context": context, "eight": eight})

        @block.tensor
        def _(pe):
            def project(tt):
                if tt == 0:
                    pe.wait_ge(s["in_x"], 16)
                    pe.wait_ge(s["in_w"], 16)
                else:
                    pe.wait_ge(s["qkv_used"], tt)
                for dst, lo, n in ((bG[0], 0, D), (bG[1], D, 2 * DKV)):
                    for k in range(KD):
                        last = nc.tensor.matmul(dst[:, 0:n], xT_sb[:, k, tt * P:(tt + 1) * P],
                                                wqkv[:, k, lo:lo + n], start=(k == 0), stop=(k == KD - 1))
                last.then_inc(s["qkv_ready"], 1)
                pe.wait_ge(s["slots_ready"], NSLOTS * (tt + 1))
                if tt == QT:
                    pe.wait_ge(s["early_copied"], 2 * GU)
                n = NQK // 8
                for j in range(n):
                    e = tt * n + j
                    if e >= 2:
                        pe.wait_ge(s["heads_copied"], e - 1)
                    bank = bT[e % 2][:].bitcast(BF16)
                    for h in range(8):
                        last = nc.tensor.transpose(bank[:, h * P:(h + 1) * P],
                                                   nat[:, 8 * j + h].rearrange("p s d -> p (s d)"), identb[:])
                    last.then_inc(s["heads_ready"], 1)

            def context(b):
                pe.wait_ge(s["ctx_ready"], 4 * (b + 1))
                if b == 1:
                    pe.wait_ge(s["cadd_ready"], 1)
                for k in range(KD):
                    last = nc.tensor.matmul(bD[:], onesb[:], ctx_q[:, b, k, :], start=(k == 0), stop=(k == KD - 1))
                last.then_inc(s["colsum_ready"], 1)

            def scores(u, g):
                b, half, n = u // HALVES, u % HALVES, u * GU + g
                kk = qst[:, H + half * GU + g, :]
                if g == 0 and half == 0:
                    pe.wait_ge(s["heads_copied"], (b + 1) * QT * NQK // 8)
                for pair in range(REP // 2):
                    bank = bS[(3 * n + pair) % 2]
                    if n >= 1 and pair == 0:
                        pe.wait_ge(s["late_used"], n * REP)
                    if n >= 1 and pair == 1:
                        pe.wait_ge(s["early_exp"], n)
                    for j in range(2):
                        q = qst[:, half * HU + g * REP + 2 * pair + j, :]
                        nc.tensor.matmul(bank[:, j * SEQ:(j + 1) * SEQ], q[:, P:SEQ], kk, start=True, stop=False,
                                         skip_group_check=True)
                        last = nc.tensor.matmul(bank[:, j * SEQ + P:(j + 1) * SEQ], identb[:], causal[:], start=False,
                                                stop=True, skip_group_check=True)
                    last.then_inc(s["late_ready"], 1)
                bank = bS[(3 * n + 2) % 2]
                pe.wait_ge(s["late_used"], n * REP + 2)
                for j in range(REP):
                    q = qst[:, half * HU + g * REP + j, :]
                    nc.tensor.matmul(bank[:, j * P:(j + 1) * P], q[:, 0:P], kk[:, 0:P], start=True, stop=False,
                                     skip_group_check=True)
                    last = nc.tensor.matmul(bank[:, j * P:(j + 1) * P], identb[:], causal[:], start=False, stop=True,
                                            skip_group_check=True)
                last.then_inc(s["early_ready"], 1)

            def early_values(u, g):
                b, half, n = u // HALVES, u % HALVES, u * GU + g
                pe.wait_ge(s["early_exp"], n + 1)
                if n >= 1:
                    pe.wait_ge(s["early_copied"], n)
                if n == 0:
                    pe.wait_ge(s["heads_copied"], QT * NQK // 8)
                if u == 2:
                    pe.wait_ge(s["heads_copied"], B * QT * NQK // 8)
                if u >= 2:
                    pe.wait_ge(s["late_copied"], QT * GU * (u - 1))
                for j in range(REP):
                    last = nc.tensor.transpose(bT[1][:, j * P:(j + 1) * P], EL[:, g * REP + j, :], identf)
                last.then_inc(s["early_turned"], 1)
                pe.wait_ge(s["early_copied"], n + 1)
                if g == 0 and u >= 1:
                    pe.wait_ge(s["early_norm"], u)
                if g == 0 and u >= 2:
                    pe.wait_ge(s["late_norm"], u - 1)
                for j in range(REP):
                    c = (g * REP + j) * VC
                    last = nc.tensor.matmul(bO[:, c:c + VC], ptL[:, j, :], vaug[:, b, 0, half * GU + g, :],
                                            start=True, stop=True)
                last.then_inc(s["early_pv"], 1)

            def pick(u):
                pe.wait_ge(s["flag_ready"], u + 1)
                pe.wait_ge(s["early_norm"], min(u + 2, NU))
                if u >= 1:
                    pe.wait_ge(s["late_norm"], u)
                nc.tensor.matmul(bO[0:1, 0:HU], onesf[:], temp["flag"][:], start=True,
                                 stop=True).then_inc(s["flag_summed"], 1)

            def late_values(u, g):
                b, half, n = u // HALVES, u % HALVES, u * GU + g
                pe.wait_ge(s["late_prob"], n * REP + REP)
                if g == 0:
                    pe.wait_ge(s["early_copied"], GU * min(u + 2, NU))
                if n == 0:
                    pe.wait_ge(s["heads_copied"], B * QT * NQK // 8)
                for kt in range(QT):
                    if n >= 1:
                        pe.wait_ge(s["late_copied"], QT * (n - 1) + kt + 1)
                    for j in range(REP):
                        last = nc.tensor.transpose(bT[kt][:, j * P:(j + 1) * P],
                                                   E[:, g * REP + j, kt * P:(kt + 1) * P], identf)
                    last.then_inc(s["late_turned"], 1)
                pe.wait_ge(s["late_copied"], QT * (n + 1))
                for j in range(REP):
                    c = (g * REP + j) * VC
                    for kt in range(QT):
                        last = nc.tensor.matmul(bO[:, c:c + VC], ptU[:, j, kt, :], vaug[:, b, kt, half * GU + g, :],
                                                start=(kt == 0), stop=(kt == QT - 1))
                last.then_inc(s["late_pv"], 1)

            turn_bank = (bD, bG[1])

            def turn(src, row, t, ident, name):
                bank = turn_bank[t][:] if ident is identf else turn_bank[t][:].bitcast(BF16)
                for k in range(KD):
                    last = nc.tensor.transpose(bank[:, k * P:(k + 1) * P], src[:, row, k * P:(k + 1) * P],
                                               ident if ident is identf else ident[:])
                last.then_inc(s[name], 1)

            def multiply(b, lhsT, rhs, copied, name):
                for t in range(QT):
                    pe.wait_ge(s[copied], QT * b + t + 1)
                    for k in range(KD):
                        last = nc.tensor.matmul(bG[t][:], lhsT[:, k, t * P:(t + 1) * P], rhs(k),
                                                start=(k == 0), stop=(k == KD - 1))
                    last.then_inc(s[name], 1)

            def out_turn(b):
                pe.wait_ge(s["late_norm"], HALVES * (b + 1))
                if b == 0:
                    pe.wait_ge(s["cadd_ready"], B)
                    pe.wait_ge(s["qkv_used"], B * QT)
                else:
                    pe.wait_ge(s["down_used"], QT * b)
                for t in range(QT):
                    turn(A, b * QT + t, t, identf, "a_turned")

            def out_project(b):
                if b == 0:
                    pe.wait_ge(s["in_wo"], 16)
                multiply(b, xt2, lambda k: wo[:, k, :], "out_copied", "out_ready")

            def cross_turn(b):
                for t in range(QT):
                    pe.wait_ge(s["quant_ready"], b * QT + t + 1)
                    turn(aq, t, t, identb, "cross_turned")

            def cross_product(b):
                multiply(b, aqT, lambda k: ctx_q[:, b, k, :], "cross_copied", "cross_ready")

            def norm_turn(b):
                for t in range(QT):
                    pe.wait_ge(s["norm_ready"], b * QT + t + 1)
                    turn(x1, t, t, identf, "x_turned")

            gate_bank = ((bG[0], bG[0]), (bG[0], bS[0]))

            def down(b, f):
                n = b * NF + f
                pe.wait_ge(s["h_ready"], n + 1)
                for t in range(QT):
                    last = nc.tensor.matmul(turn_bank[t][:], hT[:, f, t * P:(t + 1) * P], ff[n % NR][:, 2 * D:3 * D],
                                            start=(f == 0), stop=(f == NF - 1), skip_group_check=True)
                last.then_inc(s["ff_used"], 1)

            def hidden(b, f):
                n = b * NF + f
                if f == 0:
                    pe.wait_ge(s["x_copied"], QT * (b + 1))
                pe.wait_ge(in_ff[n % NR], 16 * (n // NR + 1))
                if b == 0 and f >= 1:
                    pe.wait_ge(s["h_ready"], n)
                if b == 1 and f >= 2:
                    pe.wait_ge(s["h_ready"], n - 1)
                for j in range(2):
                    for k in range(KD):
                        last = nc.tensor.matmul(gate_bank[b][f % 2][:, j * SEQ:(j + 1) * SEQ],
                                                ff[n % NR][:, j * D + k * P:j * D + (k + 1) * P], xt2[:, k, :],
                                                start=(k == 0), stop=(k == KD - 1))
                last.then_inc(s["gate_up_ready"], 1)
                if f >= 1:
                    down(b, f - 1)

            def finish(b):
                down(b, NF - 1)

            pe.wait_ge(s["cst_ready"], 4)
            walk({"project": project, "context": context, "scores": scores, "early_values": early_values,
                  "pick": pick, "late_values": late_values, "out_turn": out_turn, "out_project": out_project,
                  "cross_turn": cross_turn, "cross_product": cross_product, "norm_turn": norm_turn,
                  "hidden": hidden, "finish": finish})

        @block.scalar
        def _(act):
            def project(tt):
                t, n = tt % QT, NQK // 8
                for j in range(n):
                    e = tt * n + j
                    act.wait_ge(s["heads_ready"], e + 1)
                    nc.scalar.activation(qst[:, 8 * j:8 * j + 8, t * P:(t + 1) * P],
                                         bT[e % 2][:].bitcast(BF16).rearrange("p (h t) -> p h t", h=8),
                                         ACT.Copy).then_inc(s["heads_copied"], 1)

            def context(b):
                act.wait_ge(s["colsum_ready"], b + 1)
                nc.scalar.activation(cadd[:, b, :], bD[:], ACT.Identity, bias=zc[:, 2:3],
                                     scale=zc[:, 0:1]).then_inc(s["cadd_ready"], 1)

            def scores(u, g):
                n = u * GU + g
                act.wait_ge(s["early_ready"], n + 1)
                act.wait_ge(s["nmax_ready"], 2 * n + 2)
                if u >= 1:
                    act.wait_ge(s["early_turned"], n - GU + 1)
                for j in range(REP):
                    h = g * REP + j
                    last = nc.scalar.activation(EL[:, h, :], bS[(3 * n + 2) % 2][:, j * P:(j + 1) * P], ACT.Exp,
                                                bias=nmax[:, u % 2, 0, h:h + 1], scale=SCALE)
                last.then_inc(s["early_exp"], 1)

            def early_values(u, g):
                n = u * GU + g
                act.wait_ge(s["early_turned"], n + 1)
                if n >= 1:
                    act.wait_ge(s["early_pv"], n)
                nc.scalar.activation(ptL[:], bT[1][:].rearrange("p (j q) -> p j q", j=REP),
                                     ACT.Copy).then_inc(s["early_copied"], 1)

            def count(u, p):
                if p == 0:
                    act.wait_ge(s["guess_ready"], u + 1)
                else:
                    act.wait_ge(s["adjusted"], (COUNTS - 1) * u + p)
                for h in range(HU):
                    c = (u * COUNTS + p) * HU + h
                    if c >= 4:
                        act.wait_ge(s["counted"], c - 3)
                    nc.scalar.activation(junk[:, c % 4, :], S[:, u % 2, h, :], ACT.Sign,
                                         bias=tiny["nt"][:, u % 2, h:h + 1],
                                         accum_out=tiny["sg"][:, u % 2, h:h + 1]).then_inc(s["counted"], 1)

            def late_exp(u):
                for h in range(HU):
                    if u == 0 and h == 0:
                        act.wait_ge(s["ctx_ready"], 4 * B)
                    if u >= 1 and h % REP == 0:
                        act.wait_ge(s["late_turned"], QT * ((u - 1) * GU + h // REP + 1))
                    nc.scalar.activation(E[:, h, :], S[:, u % 2, h, :], ACT.Exp, bias=nmax[:, u % 2, 1, h:h + 1],
                                         scale=SCALE).then_inc(s["late_exp"], 1)

            def late_values(u, g):
                n = u * GU + g
                for kt in range(QT):
                    act.wait_ge(s["late_turned"], QT * n + kt + 1)
                    if n >= 1:
                        act.wait_ge(s["late_pv"], n)
                    nc.scalar.activation(ptU[:, :, kt, :], bT[kt][:].rearrange("p (j q) -> p j q", j=REP),
                                         ACT.Copy).then_inc(s["late_copied"], 1)

            turn_bank = (bD, bG[1])

            def copy(b, t, dst, turned, copied):
                act.wait_ge(s[turned], b * QT + t + 1)
                src = turn_bank[t][:] if dst is xt2 else turn_bank[t][:].bitcast(BF16)[:, 0:D]
                nc.scalar.activation(dst[:, :, t * P:(t + 1) * P], src.rearrange("p (k q) -> p k q", k=KD),
                                     ACT.Copy).then_inc(s[copied], 1)

            def out_turn(b):
                for t in range(QT):
                    copy(b, t, xt2, "a_turned", "out_copied")

            def cross_turn(b):
                for t in range(QT):
                    copy(b, t, aqT, "cross_turned", "cross_copied")

            def norm_turn(b):
                for t in range(QT):
                    copy(b, t, xt2, "x_turned", "x_copied")

            gate_bank = ((bG[0], bG[0]), (bG[0], bS[0]))

            def hidden(b, f):
                n = b * NF + f
                act.wait_ge(s["gate_up_ready"], n + 1)
                if n >= 2:
                    act.wait_ge(s["h_ready"], n - 1)
                nc.scalar.activation(g_sb[:, f % 2, :], gate_bank[b][f % 2][:, 0:SEQ], ACT.Tanh,
                                     scale=gate_half[:, f:f + 1]).then_inc(s["gate_done"], 1)

            act.wait_ge(s["scale_ready"], 1)
            walk({"project": project, "context": context, "scores": scores, "early_values": early_values,
                  "count": count, "late_exp": late_exp, "late_values": late_values, "out_turn": out_turn,
                  "cross_turn": cross_turn, "norm_turn": norm_turn, "hidden": hidden})

        @block.vector
        def _(dve):
            steps = [0]
            v = nc.vector

            def done(ins):
                steps[0] += 1
                ins.then_inc(s["dve"], 1)
                dve.wait_ge(s["dve"], steps[0])

            def pair(*instructions):
                for ins in instructions:
                    steps[0] += 1
                    ins().then_inc(s["dve"], 1)
                dve.wait_ge(s["dve"], steps[0])

            def signal(ins, name, count):
                ins.then_inc(s[name], 1)
                dve.wait_ge(s[name], count)

            def project(tt):
                b, t = tt // QT, tt % QT
                dve.wait_ge(s["qkv_ready"], tt + 1)
                hf = HD // 2
                for a, (lo, n, src) in enumerate(((0, H, bG[0][:]), (H, HKV, bG[1][:, 0:DKV]))):
                    src = src.rearrange("p (h d) -> p h d", d=HD)

                    def table(r, c0, c1):
                        return rope_sb[:, t, a, r:r + 1, c0:c1].broadcast_to([P, n, c1 - c0])

                    pair(lambda: v.tensor_tensor(rot[:, lo:lo + n, :], src, table(0, 0, HD), ALU.mult),
                         lambda: v.tensor_tensor(rot2[:, lo:lo + n, 0:hf], src[:, :, hf:HD], table(1, 0, hf), ALU.mult),
                         lambda: v.tensor_tensor(rot2[:, lo:lo + n, hf:HD], src[:, :, 0:hf], table(1, hf, HD), ALU.mult))
                signal(v.tensor_copy(vaug[:, b, t, :, 0:HD], bG[1][:, DKV:2 * DKV].rearrange("p (h d) -> p h d", d=HD)),
                       "qkv_used", tt + 1)
                done(v.tensor_tensor(rot[:], rot[:], rot2[:], ALU.add))
                if tt >= 1:
                    dve.wait_ge(s["slots_ready"], NSLOTS * tt)
                done(v.tensor_copy(parts[:, :, 0, :], rot[:]))
                done(v.tensor_tensor(rot[:], rot[:], parts[:, :, 0, :], ALU.subtract))
                done(v.tensor_copy(parts[:, :, 1, :], rot[:]))
                signal(v.tensor_tensor(parts[:, :, 2, :], rot[:], parts[:, :, 1, :], ALU.subtract),
                       "parts_ready", tt + 1)

            def scores(u, g):
                n = u * GU + g
                hs = slice(g * REP, (g + 1) * REP)
                for j in range(REP):
                    h = g * REP + j
                    if j % 2 == 0:
                        dve.wait_ge(s["late_ready"], 2 * n + j // 2 + 1)
                    v.tensor_scalar(S[:, u % 2, h, :], bS[(3 * n + j // 2) % 2][:, j % 2 * SEQ:(j % 2 + 1) * SEQ], 1.0,
                                    None, ALU.mult, ALU.max, accum_out=smax[:, 1, h:h + 1]).then_inc(s["late_used"], 1)
                dve.wait_ge(s["late_used"], REP * (n + 1))
                v.tensor_scalar(nmax[:, u % 2, 1, hs], smax[:, 1, hs], -SCALE, None,
                                ALU.mult).then_inc(s["nmax_ready"], 1)
                dve.wait_ge(s["early_ready"], n + 1)
                done(v.tensor_reduce(smax[:, 0, hs], bS[(3 * n + 2) % 2][:].rearrange("p (j k) -> p j k", j=REP),
                                     AX_X, ALU.max))
                signal(v.tensor_scalar(nmax[:, u % 2, 0, hs], smax[:, 0, hs], -SCALE, None, ALU.mult),
                       "nmax_ready", 2 * n + 2)

            def normalise(u, t, name):
                b, half = u // HALVES, u % HALVES
                o = bO[:, 0:HU * VC].rearrange("p (h c) -> p h c", c=VC)
                done(v.reciprocal(rsum[:], o[:, :, HD]))
                dst = A[:, b * QT + t, half * HU * HD:(half + 1) * HU * HD].rearrange("p (h d) -> p h d", d=HD)
                ins = v.tensor_tensor(dst, o[:, :, 0:HD],
                                      rsum[:].rearrange("p (h d) -> p h d", d=1).broadcast_to([P, HU, HD]), ALU.mult)
                signal(ins, name, u + 1)

            def early_norm(u):
                dve.wait_ge(s["early_pv"], GU * (u + 1))
                normalise(u, 0, "early_norm")

            def late_norm(u):
                dve.wait_ge(s["late_pv"], GU * (u + 1))
                normalise(u, 1, "late_norm")

            t0, t1, t2 = temp["t0"], temp["t1"], temp["t2"]
            mag, sigma, tau, theta = temp["mag"], temp["sigma"], temp["tau"], temp["theta"]
            vm, vn, flag = temp["vm"], temp["vn"], temp["flag"]

            def per_head(t, n=8):
                return t[:].rearrange("p (h d) -> p h d", d=1).broadcast_to([P, HU, n])

            def guess(u):
                nt, kk = tiny["nt"][:, u % 2], tiny["kk"][:, u % 2]
                pair(*[lambda h=h: v.bn_stats(st[:, h, :], S[:, u % 2, h, 0:P]) for h in range(HU)])
                pair(lambda: v.tensor_tensor(t0[:], st[:, :, 1], st[:, :, 4], ALU.add),
                     lambda: v.tensor_tensor(t1[:], st[:, :, 1], st[:, :, 4], ALU.subtract),
                     lambda: v.tensor_tensor(t2[:], st[:, :, 2], st[:, :, 5], ALU.add))
                done(v.tensor_tensor(t1[:], t1[:], t1[:], ALU.mult))
                done(v.scalar_tensor_tensor(out=t1[:], in0=t1[:], scalar=P / 4.0, in1=t2[:], op0=ALU.mult, op1=ALU.add))
                done(v.tensor_scalar(t1[:], t1[:], 1.0 / P, None, ALU.mult))
                done(v.tensor_scalar(t2[:].bitcast(I32), t1[:].bitcast(I32), 0.5, SQRT_BITS, ALU.mult, ALU.add))
                pair(lambda: v.tensor_scalar(kk, t2[:], k_unit, None, ALU.mult),
                     lambda: v.tensor_scalar(t2[:], t2[:], z_neg, None, ALU.mult))
                signal(v.scalar_tensor_tensor(out=nt, in0=t0[:], scalar=-0.5, in1=t2[:], op0=ALU.mult, op1=ALU.add),
                       "guess_ready", u + 1)

            def adjust(u, p):
                nt, kk, sg = tiny["nt"][:, u % 2], tiny["kk"][:, u % 2], tiny["sg"][:, u % 2]
                old, size = tiny["sg_old"][:, u % 2], tiny["size"][:, u % 2]
                dve.wait_ge(s["counted"], HU * (COUNTS * u + p + 1))
                if p == 1:
                    done(v.tensor_tensor(t0[:], old, sg, ALU.subtract))
                    done(v.scalar_tensor_tensor(out=t0[:], in0=t0[:], scalar=-1.0, in1=t0[:], op0=ALU.mult, op1=ALU.max))
                    done(v.tensor_scalar(t0[:], t0[:], 2.0, None, ALU.add))
                    done(v.reciprocal(t1[:], t0[:]))
                    done(v.scalar_tensor_tensor(out=t1[:], in0=size, scalar=2.0, in1=t1[:], op0=ALU.add, op1=ALU.mult))
                    done(v.tensor_tensor(kk, kk, t1[:], ALU.mult))
                pair(lambda: v.scalar_tensor_tensor(out=size, in0=sg, scalar=-1.0, in1=sg, op0=ALU.mult, op1=ALU.max),
                     lambda: v.tensor_tensor(t1[:], sg, kk, ALU.mult),
                     lambda: v.tensor_copy(old, sg))
                done(v.scalar_tensor_tensor(out=t2[:], in0=size, scalar=2.0 * SLACK, in1=t1[:], op0=ALU.is_gt,
                                            op1=ALU.mult))
                signal(v.tensor_tensor(nt, nt, t2[:], ALU.subtract), "adjusted", (COUNTS - 1) * u + p + 1)

            def aim(u):
                nt, sg, size = tiny["nt"][:, u % 2], tiny["sg"][:, u % 2], tiny["size"][:, u % 2]
                dve.wait_ge(s["counted"], HU * COUNTS * (u + 1))
                pair(lambda: v.tensor_scalar(t0[:], sg, 0.5, 0.5, ALU.mult, ALU.add),
                     lambda: v.tensor_scalar(t1[:], sg, 0.0, 2.0, ALU.is_lt, ALU.mult),
                     lambda: v.scalar_tensor_tensor(out=size, in0=sg, scalar=-1.0, in1=sg, op0=ALU.mult, op1=ALU.max))
                pair(lambda: v.scalar_tensor_tensor(out=mag[:], in0=t0[:], scalar=-1.0, in1=t0[:], op0=ALU.mult,
                                                    op1=ALU.max),
                     lambda: v.tensor_scalar(sigma[:], t1[:], -1.0, None, ALU.add))
                signal(v.scalar_tensor_tensor(out=tau[:], in0=sigma[:], scalar=-1.0, in1=nt, op0=ALU.mult, op1=ALU.mult),
                       "aimed", u + 1)

            def eight(u, h):
                n = u * HU + h

                def top(h):
                    v.max(V[:, h, :], W[:, (u * HU + h) % 3, :]).then_inc(s["top_made"], 1)

                dve.wait_ge(s["z_made"], n + 1)
                if n >= 3:
                    dve.wait_ge(s["top_made"], n - 2)
                z = Z[:, h % 4, :]
                v.scalar_tensor_tensor(out=W[:, n % 3, :], in0=z, scalar=tau[:, h:h + 1], in1=z, op0=ALU.is_gt,
                                       op1=ALU.subtract, reverse1=True).then_inc(s["w_made"], 1)
                if h >= 1:
                    dve.wait_ge(s["w_made"], n)
                    top(h - 1)
                if h == HU - 1:
                    dve.wait_ge(s["w_made"], n + 1)
                    top(h)

            def pick(u):
                dve.wait_ge(s["top_made"], HU * (u + 1))
                size = tiny["size"][:, u % 2]
                place = places.rearrange("p (a e) -> p a e", a=1).broadcast_to([P, HU, 8])
                pair(lambda: v.tensor_tensor(hot[:], place, per_head(mag), ALU.is_equal),
                     lambda: v.tensor_tensor(t0[:], mag[:], sigma[:], ALU.add),
                     lambda: v.tensor_tensor(flag[:], V[:, :, 0], tau[:], ALU.is_equal))
                pair(lambda: v.tensor_tensor(hot[:], hot[:], V[:], ALU.mult),
                     lambda: v.tensor_tensor(hot2[:], place, per_head(t0), ALU.is_equal))
                pair(lambda: v.tensor_reduce(vm[:], hot[:], AX_X, ALU.add),
                     lambda: v.tensor_tensor(hot2[:], hot2[:], V[:], ALU.mult),
                     lambda: v.scalar_tensor_tensor(out=t1[:], in0=size, scalar=2.0 * SLACK, in1=flag[:], op0=ALU.is_gt,
                                                    op1=ALU.max))
                pair(lambda: v.tensor_reduce(vn[:], hot2[:], AX_X, ALU.add),
                     lambda: v.tensor_tensor(theta[:], sigma[:], vm[:], ALU.mult))
                done(v.tensor_tensor(t2[:], vm[:], vn[:], ALU.is_equal))
                signal(v.tensor_tensor(flag[:], t1[:], t2[:], ALU.max), "flag_ready", u + 1)

            def keep(u):
                dve.wait_ge(s["late_exp"], HU * (u + 1))
                dve.wait_ge(s["flag_summed"], u + 1)
                pair(lambda: v.tensor_copy(flag_row[0:1, 0:HU], bO[0:1, 0:HU]),
                     lambda: v.tensor_reduce(flag_sum[0:1, :], bO[0:1, 0:HU], AX_X, ALU.add))
                done(v.tensor_copy(flag_any[0:1, :], flag_sum[0:1, :]))
                flagged = dve.value_load(flag_any[0:1, :])
                with dve.If(flagged > 0):
                    with dve.Fori(0, HU) as h:
                        rows = dve.value_load(flag_row[0:1, bass.ds(h, 1)])
                        with dve.If(rows > 0):
                            head = S[:, u % 2, bass.ds(h, 1), :]
                            v.tensor_copy(plain[:], head)
                            dve.drain()
                            v.max(m8[:], plain[:, 0])
                            dve.drain()
                            v.match_replace(taken[:, 0], m8[:], plain[:, 0], TAKEN)
                            dve.drain()
                            with dve.Fori(0, ROUNDS - 1) as _:
                                v.max(m8[:], taken[:, 0])
                                dve.drain()
                                v.match_replace(taken[:, 0], m8[:], taken[:, 0], TAKEN)
                                dve.drain()
                            v.tensor_tensor(head, taken[:], plain[:], ALU.not_equal)
                            v.tensor_scalar(theta[:, bass.ds(h, 1)], theta[:, bass.ds(h, 1)], 0.0, 0.5, ALU.mult,
                                            ALU.add)
                            dve.drain()
                for h in range(HU):
                    v.scalar_tensor_tensor(out=E[:, h, :], in0=S[:, u % 2, h, :], scalar=theta[:, h:h + 1],
                                           in1=E[:, h, :], op0=ALU.is_ge, op1=ALU.mult).then_inc(s["late_prob"], 1)
                dve.wait_ge(s["late_prob"], HU * (u + 1))

            def norm_scale():
                done(v.tensor_scalar(var[:], mv[:, :, 1], EPS, None, ALU.add))
                done(v.tensor_scalar(rstd[:].bitcast(I32), var[:].bitcast(I32), -0.5, RSQRT_BITS, ALU.mult, ALU.add))
                for _ in range(3):
                    done(v.tensor_tensor(sq[:], rstd[:], rstd[:], ALU.mult))
                    done(v.scalar_tensor_tensor(out=sq[:], in0=sq[:], scalar=-0.5, in1=var[:], op0=ALU.mult, op1=ALU.mult))
                    done(v.scalar_tensor_tensor(out=rstd[:], in0=sq[:], scalar=1.5, in1=rstd[:], op0=ALU.add,
                                                op1=ALU.mult))

            def layer_norm():
                pair(*[lambda t=t: v.bn_stats(st6[:, t, :], r1[:, t, :]) for t in range(QT)])
                pair(*[lambda t=t: v.bn_aggr(mv[:, t, :], st6[:, t, :]) for t in range(QT)])
                norm_scale()

            def normed(t):
                return v.tensor_scalar(x1[:, t, :], r1[:, t, :], mv[:, t, 0:1], rstd[:, t:t + 1],
                                       ALU.subtract, ALU.mult)

            def out_project(b):
                if b == 0:
                    dve.wait_ge(s["in_tok"], 32)
                for t in range(QT):
                    dve.wait_ge(s["out_ready"], b * QT + t + 1)
                    done(v.tensor_tensor(r1[:, t, :], bG[t][:], x_sb[:, b * QT + t, :], ALU.add))

            def norm_quantise(b):
                if b >= 1:
                    dve.wait_ge(s["out_done"], 16 * b)
                layer_norm()
                pair(*[lambda t=t: normed(t) for t in range(QT)])
                both = slice(0, QT)
                done(v.tensor_scalar(r1[:, both], x1[:, both], inv[:, 0:1], sc[:, 1:2], ALU.mult, ALU.add))
                done(v.tensor_scalar(r1[:, both], r1[:, both], 0.0, QMAX, ALU.max, ALU.min))
                done(v.tensor_scalar(r1[:, both], r1[:, both], MAGIC, None, ALU.add))
                for t in range(QT):
                    v.tensor_scalar(aq[:, t, :], r1[:, t, :], -(MAGIC + QMID), None, ALU.add, ALU.add,
                                    accum_out=arow[:, t:t + 1]).then_inc(s["quant_ready"], 1)
                dve.wait_ge(s["quant_ready"], QT * (b + 1))
                done(v.tensor_scalar(arow[:], arow[:], zc[:, 1:2], None, ALU.mult))

            def cross_product(b):
                dve.wait_ge(s["cadd_ready"], b + 1)
                for t in range(QT):
                    dve.wait_ge(s["cross_ready"], b * QT + t + 1)
                    done(v.scalar_tensor_tensor(out=r1[:, t, :], in0=bG[t][:], scalar=arow[:, t:t + 1],
                                                in1=cadd[:, b, :], op0=ALU.add, op1=ALU.add))
                pair(*[lambda t=t: v.scalar_tensor_tensor(out=r1[:, t, :], in0=r1[:, t, :], scalar=zc[:, 3:4],
                                                          in1=x1[:, t, :], op0=ALU.mult, op1=ALU.add)
                       for t in range(QT)])

            def norm_turn(b):
                layer_norm()
                for t in range(QT):
                    normed(t).then_inc(s["norm_ready"], 1)
                dve.wait_ge(s["norm_ready"], QT * (b + 1))

            gate_bank = ((bG[0], bG[0]), (bG[0], bS[0]))

            def hidden(b, f):
                n = b * NF + f
                bank = gate_bank[b][f % 2]
                dve.wait_ge(s["gate_done"], n + 1)
                done(v.scalar_tensor_tensor(out=g_sb[:, f % 2, :], in0=g_sb[:, f % 2, :], scalar=1.0,
                                            in1=bank[:, 0:SEQ], op0=ALU.add, op1=ALU.mult))
                signal(v.scalar_tensor_tensor(out=hT[:, f, :], in0=g_sb[:, f % 2, :], scalar=both_half[:, f:f + 1],
                                              in1=bank[:, SEQ:2 * SEQ], op0=ALU.mult, op1=ALU.mult), "h_ready", n + 1)

            def finish(b):
                dve.wait_ge(s["ff_used"], NF * (b + 1))
                for t, bank in enumerate((bD, bG[1])):
                    v.tensor_tensor(r1[:, t, :], bank[:], ds[:], ALU.mult).then_inc(s["down_used"], 1)
                dve.wait_ge(s["down_used"], QT * (b + 1))
                pair(*[lambda t=t: v.tensor_tensor(r1[:, t, :], r1[:, t, :], x1[:, t, :], ALU.add) for t in range(QT)])
                layer_norm()
                for t in range(QT):
                    normed(t).then_inc(s["y_ready"], 1)
                dve.wait_ge(s["y_ready"], QT * (b + 1))

            dve.wait_ge(s["in_cst"], 48)
            signal(v.tensor_copy(identb[:], cst[:, 0:P]), "cst_ready", 1)
            signal(v.tensor_copy(causal[:], cst[:, P:2 * P]), "cst_ready", 2)
            signal(v.memset(onesb[:], 1.0), "cst_ready", 3)
            signal(v.memset(onesf[:], 1.0), "cst_ready", 4)
            done(v.memset(vaug[:], 1.0))
            done(v.reciprocal(inv[:], sc[:]))
            done(v.tensor_scalar(zc[:, 0:1], sc[:, 1:2], QMID, -1.0, ALU.subtract, ALU.mult))
            done(v.tensor_scalar(zc[:, 1:2], sc[:, 3:4], QMID, -1.0, ALU.subtract, ALU.mult))
            done(v.tensor_tensor(zc[:, 2:3], zc[:, 0:1], zc[:, 1:2], ALU.mult))
            done(v.tensor_scalar(zc[:, 2:3], zc[:, 2:3], float(D), None, ALU.mult))
            signal(v.tensor_tensor(zc[:, 3:4], sc[:, 0:1], sc[:, 2:3], ALU.mult), "scale_ready", 1)
            dve.wait_ge(s["in_gus"], 16)
            done(v.tensor_scalar(gate_half[:], gus_sb[:, 0, :], 0.5, None, ALU.mult))
            done(v.tensor_tensor(both_half[:], gate_half[:], gus_sb[:, 1, :], ALU.mult))
            walk({"project": project, "scores": scores, "early_norm": early_norm, "guess": guess, "adjust": adjust,
                  "aim": aim, "eight": eight, "pick": pick, "keep": keep, "late_norm": late_norm,
                  "out_project": out_project, "norm_quantise": norm_quantise, "cross_product": cross_product,
                  "norm_turn": norm_turn, "hidden": hidden, "finish": finish})



def normal_quantile(p):
    lo, hi = -8.0, 8.0
    for _ in range(60):
        mid = (lo + hi) / 2
        lo, hi = (mid, hi) if (1 + math.erf(mid / math.sqrt(2))) / 2 < p else (lo, mid)
    return (lo + hi) / 2


def kernel(**inputs):
    import concourse.bacc as bacc
    from concourse.bass_utils import run_bass_kernel_spmd

    a = {k: np.asarray(v) for k, v in inputs.items()}

    freq = 1.0 / np.float32(THETA) ** (np.arange(0, HD, 2, dtype=np.float32) / np.float32(HD))
    ang = np.outer(np.arange(SEQ, dtype=np.float32), freq).astype(np.float32)
    ang = np.concatenate([ang, ang], axis=-1)
    sign = np.concatenate([-np.ones(HD // 2), np.ones(HD // 2)]).astype(np.float32)
    table = np.stack([np.cos(ang), np.sin(ang) * sign], axis=1).astype(np.float32)
    rope = np.stack([table * np.float32(SHRINK), table], axis=1)
    causal = np.triu(np.full((P, P), MASKED, np.float32), 1)
    seen = [P + 1 + r for r in range(P)]
    z = [normal_quantile(1 - KEEP / n) for n in seen]
    z_neg = np.array([[-q] for q in z], np.float32)
    k_unit = np.array([[BOLD / (2 * n * math.exp(-q * q / 2) / math.sqrt(2 * math.pi))] for n, q in zip(seen, z)],
                      np.float32)
    places = np.broadcast_to(np.arange(8, dtype=np.float32) + np.float32(0.5), (P, 8))
    consts = np.concatenate([np.eye(P, dtype=np.float32), causal, z_neg, k_unit, places,
                             np.zeros((P, 6), np.float32)], axis=1)

    def hidden_columns(w):
        padded = np.zeros((NF * P, D), w.dtype)
        padded[:DFF] = w
        return padded.reshape(NF, P, KD, P).transpose(0, 3, 2, 1).reshape(NF, P, D)

    down = np.zeros((NF * P, D), a["L0_ffn_down_w"].dtype)
    down[:DFF] = a["L0_ffn_down_w"].T
    ffw = np.concatenate([hidden_columns(a["L0_ffn_gate_w"]), hidden_columns(a["L0_ffn_up_w"]),
                          down.reshape(NF, P, D)], axis=2)
    gus = np.zeros((2, NF * P), np.float32)
    gus[0, :DFF], gus[1, :DFF] = a["L0_ffn_gate_s"], a["L0_ffn_up_s"]
    arrays = {
        "x": a["x"],
        "xT": a["x"].reshape(B * SEQ, D).T,
        "ctx": a["ctx_4096"],
        "wqkvT": np.concatenate([a["L0_attn_Wq"], a["L0_attn_Wk"], a["L0_attn_Wv"]], axis=0).T,
        "woT": a["L0_attn_Wo"].T,
        "scal": np.concatenate([a["L0_xattn_x1_scale"], a["L0_xattn_x1_zp"],
                                a["L0_xattn_x2_scale"], a["L0_xattn_x2_zp"]]),
        "ffw": ffw,
        "gus": gus.reshape(2, NF, P).transpose(2, 0, 1),
        "down_s": a["L0_ffn_down_s"],
        "rope": rope,
        "consts": consts,
    }
    arrays = {k: np.ascontiguousarray(w) for k, w in arrays.items()}
    nc = bacc.Bacc("TRN2", target_bir_lowering=False, num_devices=1)
    args = [nc.dram_tensor(k, w.shape, mybir.dt.from_np(w.dtype), kind="ExternalInput").ap() for k, w in arrays.items()]
    out = nc.dram_tensor("out", (B, SEQ, D), F32, kind="ExternalOutput").ap()
    decoder_layer(nc, *args, out)
    result = run_bass_kernel_spmd(nc, [arrays], core_ids=[0])
    return result.results[0]["out"]
```

```python
from contextlib import ExitStack
import math

import concourse.bass as bass
from concourse import mybir
import numpy as np

P = 128
B, SEQ, D = 2, 256, 512
H, HKV, HD = 32, 8, 16
REP = H // HKV
DKV = HKV * HD
DFF = 1376
KD = D // P
NF = -(-DFF // P)
QT = SEQ // P
NQK = H + HKV
NSLOT = P // HD
NQ_SLOT = 5
NPART = 3
KEEP = 128
ROUNDS = KEEP // 8
HALVES = 2
HU = H // HALVES
NU = B * HALVES
GU = HU // REP
VC = HD + 1
NR = 3
THETA = 10000.0
SHRINK = 2.0 ** -40
SCALE = 0.25 / SHRINK
MASKED = -0.5
TAKEN = -1.0
COUNTS = 3
SLACK = 7
BOLD = 1.1
SQRT_BITS = 532487669.0
RSQRT_BITS = float(0x5F3759DF)
MAGIC = float(2 ** 23)
QMID = 128.0
QMAX = 255.0
EPS = 1e-5

F32, BF16, I32 = mybir.dt.float32, mybir.dt.bfloat16, mybir.dt.int32
ALU = mybir.AluOpType
ACT = mybir.ActivationFunctionType
AX_X = mybir.AxisListType.X



def schedule():
    out, post = [], []
    groups = range(GU)

    def add(*steps):
        out.extend(steps)

    def fill(n):
        for _ in range(min(n, len(post))):
            out.append(post.pop(0))

    def counts(u, p, gs):
        add(*[("count", u, p, g) for g in gs])

    def scored(u, g):
        add(("take", u, g))
        if g < GU - 1:
            add(("scores", u, g + 1))
        if g >= 1:
            add(("early_values", u, g - 1))
        add(("early_turn", u, g))
        if g == GU - 1:
            add(("early_values", u, g), ("early_norm", u), ("guess", u))

    add(("project", 0), ("slots", 0), ("project", 1), ("heads", 0), ("slots", 1), ("heads", 1), ("scores", 0, 0))
    for g in groups:
        scored(0, g)
    add(("context", 0), ("context", 1), ("scores", 1, 0))
    for g in groups:
        counts(0, 0, [g])
        scored(1, g)
    add(("adjust", 0, 0), ("project", QT), ("slots", QT))
    counts(0, 1, groups)
    add(("adjust", 0, 1))
    counts(0, 2, groups)
    add(("heads", QT), ("project", QT + 1), ("slots", QT + 1), ("weights", 0))
    for u in range(NU):
        nxt, more = u + 1 < NU, u + 2 < NU
        if nxt:
            counts(u + 1, 0, groups)
        add(("aim", u))
        if u == 0:
            add(("heads", QT + 1))
        if more:
            add(("scores", u + 2, 0))
        for g in groups:
            add(("late_exp", u, g))
        for h in range(12):
            add(("eight", u, h))
            if h % 2:
                fill(1)
        if nxt:
            add(("adjust", u + 1, 0))
            counts(u + 1, 1, groups)
        for h in range(12, HU):
            add(("eight", u, h))
        fill(1)
        add(("pick", u), ("keep", u))
        for g in groups:
            add(("keep_group", u, g))
            if g >= 1:
                add(("late_values", u, g - 1))
            add(("late_turn", u, g))
            if more:
                scored(u + 2, g)
            if nxt and g == 1:
                add(("adjust", u + 1, 1))
            if nxt and g >= 2:
                counts(u + 1, 2, [2 * g - 4, 2 * g - 3])
            if g % 2:
                fill(1)
        add(("late_values", u, GU - 1), ("late_norm", u))
        if u % HALVES == HALVES - 1:
            b = u // HALVES
            post = [(name, b) for name in ("out_turn", "out_project", "norm_quantise", "cross_turn", "cross_product",
                                           "norm_turn")]
            post += [("hidden", b, f) for f in range(NF)] + [("finish", b)]
    fill(len(post))
    return out


def decoder_layer(nc, x, xT, ctx, wqkvT, woT, scal, ffw, gus, down_s, rope, consts, out):
    steps_in_order = schedule()

    with ExitStack() as stack:
        def sb(name, shape, dt=F32):
            return stack.enter_context(nc.sbuf_tensor(name, shape, dt))

        def ps(name, shape, dt=F32):
            return stack.enter_context(nc.psum_tensor(name, shape, dt))

        def sem(name):
            return stack.enter_context(nc.semaphore(name))

        x_sb = sb("x_sb", [P, B * QT, D])
        front = sb("front", [P, KD * (B * SEQ + D + 2 * DKV)])
        xT_sb = front[:, 0:KD * B * SEQ].rearrange("p (k t) -> p k t", k=KD)
        wqkv = front[:, KD * B * SEQ:].rearrange("p (k n) -> p k n", k=KD)
        ff = [front[:, i * 3 * D:(i + 1) * 3 * D] for i in range(NR)]
        wo = sb("wo", [P, KD, D])
        ctx_q = sb("ctx_q", [P, B, KD, D], BF16)
        gus_sb = sb("gus_sb", [P, 2, NF])
        gate_half = sb("gate_half", [P, NF])
        both_half = sb("both_half", [P, NF])
        ds = sb("ds", [P, D])
        sc = sb("sc", [P, 4])
        inv = sb("inv", [P, 4])
        zc = sb("zc", [P, 4])
        rope_sb = sb("rope_sb", [P, QT, 2, 2, HD])
        cst = sb("cst", [P, 2 * P + 16])
        identf = cst[:, 0:P]
        z_neg, k_unit = cst[:, 2 * P:2 * P + 1], cst[:, 2 * P + 1:2 * P + 2]
        places = cst[:, 2 * P + 2:2 * P + 10]
        identb = sb("identb", [P, P], BF16)
        causal = sb("causal", [P, P], BF16)
        onesb = sb("onesb", [P, P], BF16)
        onesf = sb("onesf", [P, 1])
        middle = sb("middle", [P, NF * SEQ + 2 * SEQ])
        slot_floats = NQ_SLOT * H * HD // 2
        q_parts = middle[:, 0:slot_floats].bitcast(BF16).rearrange("p (h s d) -> p h s d", h=H, s=NQ_SLOT)
        k_slots = middle[:, slot_floats:slot_floats + DKV * NSLOT // 2].bitcast(BF16).rearrange(
            "p (h s d) -> p h s d", h=HKV, s=NSLOT)
        k_parts = sb("k_parts", [P, HKV, NPART, HD], BF16)
        hT = middle[:, 0:NF * SEQ].rearrange("p (f t) -> p f t", f=NF)
        g_sb = middle[:, NF * SEQ:NF * SEQ + 2 * SEQ].rearrange("p (a t) -> p a t", a=2)
        rot = sb("rot", [P, NQK, HD])
        rot2 = sb("rot2", [P, NQK, HD])
        qst = sb("qst", [P, NQK, SEQ], BF16)
        vaug = sb("vaug", [P, B, QT, HKV, VC])
        S = sb("S", [P, 2, HU, SEQ])
        E = sb("E", [P, HU, SEQ])
        EL = sb("EL", [P, HU, P])
        Z = sb("Z", [P, 4, SEQ])
        W = sb("W", [P, 3, SEQ])
        m8 = sb("m8", [P, 8])
        plain = sb("plain", [P, 1, SEQ])
        taken = sb("taken", [P, 1, SEQ])
        V = sb("V", [P, HU, 8])
        hot = sb("hot", [P, HU, 8])
        hot2 = sb("hot2", [P, HU, 8])
        st = sb("st", [P, HU, 6])
        smax = sb("smax", [P, QT, HU])
        nmax = sb("nmax", [P, 2, QT, HU])
        tiny = {n: sb(n, [P, 2, HU]) for n in ("nt", "kk", "sg", "sg_old", "size")}
        temp = {n: sb(n, [P, HU]) for n in ("t0", "t1", "t2", "mag", "sigma", "tau", "theta", "vm", "vn", "flag")}
        flag_row = sb("flag_row", [P, 2 * HU], I32)
        flag_sum = sb("flag_sum", [P, 1])
        flag_any = sb("flag_any", [P, 1], I32)
        ptL = sb("ptL", [P, REP, P])
        ptU = sb("ptU", [P, 2, REP, QT, P])
        rsum = sb("rsum", [P, HU])
        A = sb("A", [P, B * QT, D])
        junk = sb("junk", [P, 4, SEQ], BF16)
        xt2 = sb("xt2", [P, KD, SEQ])
        r1 = sb("r1", [P, QT, D])
        x1 = sb("x1", [P, QT, D])
        aq = sb("aq", [P, QT, D], BF16)
        aqT = sb("aqT", [P, KD, SEQ], BF16)
        cadd = sb("cadd", [P, B, D])
        arow = sb("arow", [P, QT])
        st6 = sb("st6", [P, QT, 6])
        mv = sb("mv", [P, QT, 2])
        var = sb("var", [P, QT])
        rstd = sb("rstd", [P, QT])
        sq = sb("sq", [P, QT])

        bS = [ps("bS0", [P, 512]), ps("bS1", [P, 512])]
        bT = [ps("bT0", [P, 512]), ps("bT1", [P, 512])]
        bO = ps("bO", [P, 512])
        bG = [ps("bG0", [P, 512]), ps("bG1", [P, 512])]
        bD = ps("bD", [P, 512])

        names = """scale_ready in_gus in_x in_w in_cst in_ctx in_tok in_wo cst_ready
            dve act qkv_ready qkv_used parts_ready slots_ready heads_ready heads_copied
            late_ready late_used early_ready nmax_ready late_exp early_exp late_prob
            early_turned early_copied early_pv early_norm late_turned late_copied late_pv late_norm
            guess_ready counted adjusted aimed z_made w_made top_made flag_ready flag_summed
            a_turned out_copied out_ready quant_ready cross_turned cross_copied cross_ready
            colsum_ready cadd_ready ctx_ready norm_ready x_turned x_copied
            gate_up_ready gate_done h_ready ff_used down_ready down_used y_ready out_done""".split()
        s = {n: sem(n) for n in names}
        in_ff = [sem(f"in_ff{i}") for i in range(NR)]

        def walk(handlers):
            for step in steps_in_order:
                if step[0] in handlers:
                    handlers[step[0]](*step[1:])

        NSLOTS = 4

        def fill_slots(tt, engine, copy):
            engine.wait_ge(s["parts_ready"], 2 * (tt + 1))
            copy(q_parts[:, :, NPART:NQ_SLOT, :], q_parts[:, :, 0:2, :]).then_inc(s["slots_ready"], 1)
            for part, lo, hi in ((0, 0, 3), (1, 3, 6), (2, 6, 8)):
                src = k_parts[:, :, part:part + 1, :].broadcast_to([P, HKV, hi - lo, HD])
                copy(k_slots[:, :, lo:hi, :], src).then_inc(s["slots_ready"], 1)

        block = stack.enter_context(nc.Block())

        @block.sync
        def _(sp):
            sp.dma_start(xT_sb, xT.rearrange("(k p) t -> p k t", p=P)).then_inc(s["in_x"], 16)
            sp.dma_start(wqkv, wqkvT.rearrange("(k p) n -> p k n", p=P)).then_inc(s["in_w"], 16)
            sp.dma_start(cst[:], consts).then_inc(s["in_cst"], 16)
            sp.dma_start(rope_sb[:], rope.rearrange("(t p) a r d -> p t a r d", p=P)).then_inc(s["in_cst"], 16)
            sp.dma_start(sc[:], scal[None, :].broadcast_to([P, 4])).then_inc(s["in_cst"], 16)
            sp.dma_start(gus_sb[:], gus).then_inc(s["in_gus"], 16)
            sp.dma_start(E[:].rearrange("p (b k a) n -> p b k (a n)", b=B, k=KD),
                         ctx.rearrange("b (k p) n -> p b k n", p=P)).then_inc(s["in_ctx"], 16)
            sp.dma_start(x_sb[:], x.rearrange("b (t p) d -> p (b t) d", p=P)).then_inc(s["in_tok"], 16)
            sp.dma_start(ds[:], down_s[None, :].broadcast_to([P, D])).then_inc(s["in_tok"], 16)
            sp.dma_start(wo[:], woT.rearrange("(k p) n -> p k n", p=P)).then_inc(s["in_wo"], 16)
            for b in range(B):
                sp.wait_ge(s["y_ready"], QT * (b + 1))
                sp.dma_start(out[b].rearrange("(t p) d -> p t d", p=P), x1[:]).then_inc(s["out_done"], 16)
            sp.wait_ge(s["out_done"], 16 * B)

        @block.gpsimd
        def _(pool):
            def load(n):
                pool.dma_start(ff[n % NR], ffw[n % NF]).then_inc(in_ff[n % NR], 16)

            def slots(tt):
                if tt >= QT:
                    fill_slots(tt, pool, nc.gpsimd.tensor_copy)

            def weights(_):
                pool.wait_ge(s["qkv_ready"], B * QT)
                for n in range(NR):
                    load(n)

            def hidden(b, f):
                n = b * NF + f
                if n >= 1 and n - 1 + NR < B * NF:
                    pool.wait_ge(s["ff_used"], n)
                    load(n - 1 + NR)

            def context(b):
                if b == 0:
                    pool.wait_ge(s["in_ctx"], 16)
                    pool.wait_ge(s["scale_ready"], 1)
                c = E[:, b * HU // 2:(b + 1) * HU // 2, :].rearrange("p (k a) n -> p k (a n)", k=KD)
                base = 4 * b
                nc.gpsimd.tensor_scalar(c, c, inv[:, 2:3], sc[:, 3:4], ALU.mult, ALU.add).then_inc(s["ctx_ready"], 1)
                pool.wait_ge(s["ctx_ready"], base + 1)
                nc.gpsimd.tensor_scalar(c, c, QMAX, 0.0, ALU.min, ALU.max).then_inc(s["ctx_ready"], 1)
                pool.wait_ge(s["ctx_ready"], base + 2)
                nc.gpsimd.tensor_scalar(c, c, MAGIC, 1.0, ALU.add, ALU.mult).then_inc(s["ctx_ready"], 1)
                pool.wait_ge(s["ctx_ready"], base + 3)
                nc.gpsimd.tensor_scalar(ctx_q[:, b], c, -(MAGIC + QMID), 1.0, ALU.add,
                                        ALU.mult).then_inc(s["ctx_ready"], 1)

            def eight(u, h):
                n = u * HU + h
                if h == 0:
                    pool.wait_ge(s["aimed"], u + 1)
                if n >= 4:
                    pool.wait_ge(s["w_made"], n - 3)
                nc.gpsimd.tensor_scalar(Z[:, h % 4, :], S[:, u % 2, h, :], temp["sigma"][:, h:h + 1], 1.0,
                                        ALU.mult, ALU.mult).then_inc(s["z_made"], 1)

            walk({"slots": slots, "weights": weights, "hidden": hidden, "context": context, "eight": eight})

        @block.tensor
        def _(pe):
            def project(tt):
                if tt == 0:
                    pe.wait_ge(s["in_x"], 16)
                    pe.wait_ge(s["in_w"], 16)
                else:
                    pe.wait_ge(s["qkv_used"], tt)
                if tt == QT:
                    pe.wait_ge(s["early_exp"], 2 * GU)
                    pe.wait_ge(s["early_copied"], 2 * GU)
                for dst, lo, n in ((bG[0], 0, D), (bG[1], D, 2 * DKV)):
                    for k in range(KD):
                        last = nc.tensor.matmul(dst[:, 0:n], xT_sb[:, k, tt * P:(tt + 1) * P],
                                                wqkv[:, k, lo:lo + n], start=(k == 0), stop=(k == KD - 1))
                last.then_inc(s["qkv_ready"], 1)

            def heads(tt):
                pe.wait_ge(s["slots_ready"], NSLOTS * (tt + 1))
                n = NQK // 8
                for j in range(n):
                    e = tt * n + j
                    if e >= 2:
                        pe.wait_ge(s["heads_copied"], e - 1)
                    bank = bT[e % 2][:].bitcast(BF16)
                    for h in range(8):
                        if j < H // 8:
                            head = q_parts[:, 8 * j + h].rearrange("p s d -> p (s d)")
                            nc.tensor.transpose(bank[0:P // 2, h * P:(h + 1) * P], head[:, 0:4 * HD], identb[:])
                            last = nc.tensor.transpose(bank[P // 2:P, h * P:(h + 1) * P], head[:, HD:5 * HD],
                                                       identb[:])
                        else:
                            last = nc.tensor.transpose(bank[:, h * P:(h + 1) * P],
                                                       k_slots[:, h].rearrange("p s d -> p (s d)"), identb[:])
                    last.then_inc(s["heads_ready"], 1)

            def context(b):
                pe.wait_ge(s["ctx_ready"], 4 * (b + 1))
                if b == 0:
                    pe.wait_ge(s["early_norm"], 1)
                else:
                    pe.wait_ge(s["cadd_ready"], 1)
                for k in range(KD):
                    last = nc.tensor.matmul(bD[:], onesb[:], ctx_q[:, b, k, :], start=(k == 0), stop=(k == KD - 1))
                last.then_inc(s["colsum_ready"], 1)

            def scores(u, g):
                b, half, n = u // HALVES, u % HALVES, u * GU + g
                kk = qst[:, H + half * GU + g, :]
                if g == 0 and half == 0:
                    pe.wait_ge(s["heads_copied"], (b + 1) * QT * NQK // 8)
                for pair in range(REP // 2):
                    if n >= 1:
                        pe.wait_ge(s["late_used"], (n - 1) * REP + 2 * pair + 2)
                    for j in range(2):
                        q = qst[:, half * HU + g * REP + 2 * pair + j, :]
                        nc.tensor.matmul(bS[pair][:, j * SEQ:(j + 1) * SEQ], q[:, P:SEQ], kk, start=True, stop=False,
                                         skip_group_check=True)
                        last = nc.tensor.matmul(bS[pair][:, j * SEQ + P:(j + 1) * SEQ], identb[:], causal[:],
                                                start=False, stop=True, skip_group_check=True)
                    last.then_inc(s["late_ready"], 1)
                if g == 0:
                    pe.wait_ge(s["qkv_used"], (b + 1) * QT)
                if n >= 1:
                    pe.wait_ge(s["early_exp"], n)
                for j in range(REP):
                    q = qst[:, half * HU + g * REP + j, :]
                    nc.tensor.matmul(bG[0][:, j * P:(j + 1) * P], q[:, 0:P], kk[:, 0:P], start=True, stop=False,
                                     skip_group_check=True)
                    last = nc.tensor.matmul(bG[0][:, j * P:(j + 1) * P], identb[:], causal[:], start=False, stop=True,
                                            skip_group_check=True)
                last.then_inc(s["early_ready"], 1)

            def early_turn(u, g):
                n = u * GU + g
                pe.wait_ge(s["early_exp"], n + 1)
                if n >= 1:
                    pe.wait_ge(s["early_copied"], n)
                for j in range(REP):
                    last = nc.tensor.transpose(bG[1][:, j * P:(j + 1) * P], EL[:, g * REP + j, :], identf)
                last.then_inc(s["early_turned"], 1)

            def early_values(u, g):
                b, half, n = u // HALVES, u % HALVES, u * GU + g
                pe.wait_ge(s["early_copied"], n + 1)
                if g == 0 and u >= 1:
                    pe.wait_ge(s["early_norm"], u)
                if g == 0 and u == 1:
                    pe.wait_ge(s["cadd_ready"], B)
                for j in range(REP):
                    c = (g * REP + j) * VC
                    last = nc.tensor.matmul(bD[:, c:c + VC], ptL[:, j, :], vaug[:, b, 0, half * GU + g, :],
                                            start=True, stop=True)
                last.then_inc(s["early_pv"], 1)

            def pick(u):
                pe.wait_ge(s["flag_ready"], u + 1)
                if u >= 1:
                    pe.wait_ge(s["late_norm"], u)
                nc.tensor.matmul(bO[0:1, 0:HU], onesf[:], temp["flag"][:], start=True,
                                 stop=True).then_inc(s["flag_summed"], 1)

            def late_turn(u, g):
                n = u * GU + g
                pe.wait_ge(s["late_prob"], n * REP + REP)
                if n == 0:
                    pe.wait_ge(s["heads_copied"], B * QT * NQK // 8)
                for kt in range(QT):
                    if n >= 1:
                        pe.wait_ge(s["late_copied"], QT * (n - 1) + kt + 1)
                    for j in range(REP):
                        last = nc.tensor.transpose(bT[kt][:, j * P:(j + 1) * P],
                                                   E[:, g * REP + j, kt * P:(kt + 1) * P], identf)
                    last.then_inc(s["late_turned"], 1)

            def late_values(u, g):
                b, half, n = u // HALVES, u % HALVES, u * GU + g
                pe.wait_ge(s["late_copied"], QT * (n + 1))
                for j in range(REP):
                    c = (g * REP + j) * VC
                    for kt in range(QT):
                        last = nc.tensor.matmul(bO[:, c:c + VC], ptU[:, n % 2, j, kt, :],
                                                vaug[:, b, kt, half * GU + g, :],
                                                start=(kt == 0), stop=(kt == QT - 1))
                last.then_inc(s["late_pv"], 1)

            turn_bank = (bD, bG[1])

            def turn(src, row, t, ident, name):
                bank = turn_bank[t][:] if ident is identf else turn_bank[t][:].bitcast(BF16)
                for k in range(KD):
                    last = nc.tensor.transpose(bank[:, k * P:(k + 1) * P], src[:, row, k * P:(k + 1) * P],
                                               ident if ident is identf else ident[:])
                last.then_inc(s[name], 1)

            def multiply(b, lhsT, rhs, copied, name):
                for t in range(QT):
                    pe.wait_ge(s[copied], QT * b + t + 1)
                    for k in range(KD):
                        last = nc.tensor.matmul(bG[t][:], lhsT[:, k, t * P:(t + 1) * P], rhs(k),
                                                start=(k == 0), stop=(k == KD - 1))
                    last.then_inc(s[name], 1)

            def out_turn(b):
                pe.wait_ge(s["late_norm"], HALVES * (b + 1))
                if b == 0:
                    pe.wait_ge(s["early_norm"], NU)
                    pe.wait_ge(s["early_exp"], NU * GU)
                    pe.wait_ge(s["early_copied"], NU * GU)
                else:
                    pe.wait_ge(s["down_used"], QT * b)
                for t in range(QT):
                    turn(A, b * QT + t, t, identf, "a_turned")

            def out_project(b):
                if b == 0:
                    pe.wait_ge(s["in_wo"], 16)
                multiply(b, xt2, lambda k: wo[:, k, :], "out_copied", "out_ready")

            def cross_turn(b):
                for t in range(QT):
                    pe.wait_ge(s["quant_ready"], b * QT + t + 1)
                    turn(aq, t, t, identb, "cross_turned")

            def cross_product(b):
                multiply(b, aqT, lambda k: ctx_q[:, b, k, :], "cross_copied", "cross_ready")

            def norm_turn(b):
                for t in range(QT):
                    pe.wait_ge(s["norm_ready"], b * QT + t + 1)
                    turn(x1, t, t, identf, "x_turned")

            gate_bank = ((bG[0], bG[0]), (bG[0], bS[0]))

            def down(b, f):
                n = b * NF + f
                pe.wait_ge(s["h_ready"], n + 1)
                for t in range(QT):
                    last = nc.tensor.matmul(turn_bank[t][:], hT[:, f, t * P:(t + 1) * P], ff[n % NR][:, 2 * D:3 * D],
                                            start=(f == 0), stop=(f == NF - 1), skip_group_check=True)
                last.then_inc(s["ff_used"], 1)

            def hidden(b, f):
                n = b * NF + f
                if f == 0:
                    pe.wait_ge(s["x_copied"], QT * (b + 1))
                pe.wait_ge(in_ff[n % NR], 16 * (n // NR + 1))
                if b == 0 and f >= 1:
                    pe.wait_ge(s["h_ready"], n)
                if b == 1 and f >= 2:
                    pe.wait_ge(s["h_ready"], n - 1)
                for j in range(2):
                    for k in range(KD):
                        last = nc.tensor.matmul(gate_bank[b][f % 2][:, j * SEQ:(j + 1) * SEQ],
                                                ff[n % NR][:, j * D + k * P:j * D + (k + 1) * P], xt2[:, k, :],
                                                start=(k == 0), stop=(k == KD - 1))
                last.then_inc(s["gate_up_ready"], 1)
                if f >= 1:
                    down(b, f - 1)

            def finish(b):
                down(b, NF - 1)

            pe.wait_ge(s["cst_ready"], 4)
            walk({"project": project, "heads": heads, "context": context, "scores": scores, "early_turn": early_turn,
                  "early_values": early_values, "pick": pick, "late_turn": late_turn, "late_values": late_values, "out_turn": out_turn, "out_project": out_project,
                  "cross_turn": cross_turn, "cross_product": cross_product, "norm_turn": norm_turn,
                  "hidden": hidden, "finish": finish})

        @block.scalar
        def _(act):
            def slots(tt):
                if tt < QT:
                    fill_slots(tt, act, lambda dst, src: nc.scalar.activation(dst, src, ACT.Copy))

            def heads(tt):
                t, n = tt % QT, NQK // 8
                for j in range(n):
                    e = tt * n + j
                    act.wait_ge(s["heads_ready"], e + 1)
                    nc.scalar.activation(qst[:, 8 * j:8 * j + 8, t * P:(t + 1) * P],
                                         bT[e % 2][:].bitcast(BF16).rearrange("p (h t) -> p h t", h=8),
                                         ACT.Copy).then_inc(s["heads_copied"], 1)

            def context(b):
                act.wait_ge(s["colsum_ready"], b + 1)
                nc.scalar.activation(cadd[:, b, :], bD[:], ACT.Identity, bias=zc[:, 2:3],
                                     scale=zc[:, 0:1]).then_inc(s["cadd_ready"], 1)

            def take(u, g):
                n = u * GU + g
                act.wait_ge(s["early_ready"], n + 1)
                act.wait_ge(s["nmax_ready"], 2 * n + 2)
                if u >= 1:
                    act.wait_ge(s["early_turned"], n - GU + 1)
                for j in range(REP):
                    h = g * REP + j
                    last = nc.scalar.activation(EL[:, h, :], bG[0][:, j * P:(j + 1) * P], ACT.Exp,
                                                bias=nmax[:, u % 2, 0, h:h + 1], scale=SCALE)
                last.then_inc(s["early_exp"], 1)

            def early_turn(u, g):
                n = u * GU + g
                act.wait_ge(s["early_turned"], n + 1)
                if n >= 1:
                    act.wait_ge(s["early_pv"], n)
                nc.scalar.activation(ptL[:], bG[1][:].rearrange("p (j q) -> p j q", j=REP),
                                     ACT.Copy).then_inc(s["early_copied"], 1)

            def count(u, p, g):
                if p == 0:
                    act.wait_ge(s["guess_ready"], u + 1)
                else:
                    act.wait_ge(s["adjusted"], (COUNTS - 1) * u + p)
                for h in range(g * REP, (g + 1) * REP):
                    c = (u * COUNTS + p) * HU + h
                    if c >= 4:
                        act.wait_ge(s["counted"], c - 3)
                    nc.scalar.activation(junk[:, c % 4, :], S[:, u % 2, h, :], ACT.Sign,
                                         bias=tiny["nt"][:, u % 2, h:h + 1],
                                         accum_out=tiny["sg"][:, u % 2, h:h + 1]).then_inc(s["counted"], 1)

            def late_exp(u, g):
                for h in range(g * REP, (g + 1) * REP):
                    if u == 0 and h == 0:
                        act.wait_ge(s["ctx_ready"], 4 * B)
                    if u >= 1 and h % REP == 0:
                        act.wait_ge(s["late_turned"], QT * ((u - 1) * GU + h // REP + 1))
                    nc.scalar.activation(E[:, h, :], S[:, u % 2, h, :], ACT.Exp, bias=nmax[:, u % 2, 1, h:h + 1],
                                         scale=SCALE).then_inc(s["late_exp"], 1)

            def late_turn(u, g):
                n = u * GU + g
                for kt in range(QT):
                    act.wait_ge(s["late_turned"], QT * n + kt + 1)
                    if n >= 2:
                        act.wait_ge(s["late_pv"], n - 1)
                    nc.scalar.activation(ptU[:, n % 2, :, kt, :], bT[kt][:].rearrange("p (j q) -> p j q", j=REP),
                                         ACT.Copy).then_inc(s["late_copied"], 1)

            turn_bank = (bD, bG[1])

            def copy(b, t, dst, turned, copied):
                act.wait_ge(s[turned], b * QT + t + 1)
                src = turn_bank[t][:] if dst is xt2 else turn_bank[t][:].bitcast(BF16)[:, 0:D]
                nc.scalar.activation(dst[:, :, t * P:(t + 1) * P], src.rearrange("p (k q) -> p k q", k=KD),
                                     ACT.Copy).then_inc(s[copied], 1)

            def out_turn(b):
                for t in range(QT):
                    copy(b, t, xt2, "a_turned", "out_copied")

            def cross_turn(b):
                for t in range(QT):
                    copy(b, t, aqT, "cross_turned", "cross_copied")

            def norm_turn(b):
                for t in range(QT):
                    copy(b, t, xt2, "x_turned", "x_copied")

            gate_bank = ((bG[0], bG[0]), (bG[0], bS[0]))

            def hidden(b, f):
                n = b * NF + f
                act.wait_ge(s["gate_up_ready"], n + 1)
                if n >= 2:
                    act.wait_ge(s["h_ready"], n - 1)
                nc.scalar.activation(g_sb[:, f % 2, :], gate_bank[b][f % 2][:, 0:SEQ], ACT.Tanh,
                                     scale=gate_half[:, f:f + 1]).then_inc(s["gate_done"], 1)

            act.wait_ge(s["scale_ready"], 1)
            walk({"slots": slots, "heads": heads, "context": context, "take": take, "early_turn": early_turn,
                  "count": count, "late_exp": late_exp, "late_turn": late_turn, "out_turn": out_turn,
                  "cross_turn": cross_turn, "norm_turn": norm_turn, "hidden": hidden})

        @block.vector
        def _(dve):
            steps = [0]
            v = nc.vector

            def done(ins):
                steps[0] += 1
                ins.then_inc(s["dve"], 1)
                dve.wait_ge(s["dve"], steps[0])

            def pair(*instructions):
                for ins in instructions:
                    steps[0] += 1
                    ins().then_inc(s["dve"], 1)
                dve.wait_ge(s["dve"], steps[0])

            def signal(ins, name, count):
                ins.then_inc(s[name], 1)
                dve.wait_ge(s[name], count)

            def project(tt):
                b, t = tt // QT, tt % QT
                dve.wait_ge(s["qkv_ready"], tt + 1)
                hf = HD // 2
                for a, (lo, n, src) in enumerate(((0, H, bG[0][:]), (H, HKV, bG[1][:, 0:DKV]))):
                    src = src.rearrange("p (h d) -> p h d", d=HD)

                    def table(r, c0, c1):
                        return rope_sb[:, t, a, r:r + 1, c0:c1].broadcast_to([P, n, c1 - c0])

                    pair(lambda: v.tensor_tensor(rot[:, lo:lo + n, :], src, table(0, 0, HD), ALU.mult),
                         lambda: v.tensor_tensor(rot2[:, lo:lo + n, 0:hf], src[:, :, hf:HD], table(1, 0, hf), ALU.mult),
                         lambda: v.tensor_tensor(rot2[:, lo:lo + n, hf:HD], src[:, :, 0:hf], table(1, hf, HD), ALU.mult))
                signal(v.tensor_copy(vaug[:, b, t, :, 0:HD], bG[1][:, DKV:2 * DKV].rearrange("p (h d) -> p h d", d=HD)),
                       "qkv_used", tt + 1)
                done(v.tensor_tensor(rot[:], rot[:], rot2[:], ALU.add))
                if tt >= 1:
                    dve.wait_ge(s["heads_ready"], tt * NQK // 8)
                heads = ((rot[:, 0:H], q_parts), (rot[:, H:NQK], k_parts))
                for part in range(NPART - 1):
                    pair(*[lambda r=r, w=w: v.tensor_copy(w[:, :, part, :], r) for r, w in heads])
                    if part == 0:
                        pair(*[lambda r=r, w=w: v.tensor_tensor(r, r, w[:, :, 0, :], ALU.subtract) for r, w in heads])
                for r, w in heads:
                    v.tensor_tensor(w[:, :, 2, :], r, w[:, :, 1, :], ALU.subtract).then_inc(s["parts_ready"], 1)
                dve.wait_ge(s["parts_ready"], 2 * (tt + 1))

            def take(u, g):
                n = u * GU + g
                hs = slice(g * REP, (g + 1) * REP)
                for j in range(REP):
                    h = g * REP + j
                    if j % 2 == 0:
                        dve.wait_ge(s["late_ready"], 2 * n + j // 2 + 1)
                    v.tensor_scalar(S[:, u % 2, h, :], bS[j // 2][:, j % 2 * SEQ:(j % 2 + 1) * SEQ], 1.0,
                                    None, ALU.mult, ALU.max, accum_out=smax[:, 1, h:h + 1]).then_inc(s["late_used"], 1)
                dve.wait_ge(s["late_used"], REP * (n + 1))
                v.tensor_scalar(nmax[:, u % 2, 1, hs], smax[:, 1, hs], -SCALE, None,
                                ALU.mult).then_inc(s["nmax_ready"], 1)
                dve.wait_ge(s["early_ready"], n + 1)
                done(v.tensor_reduce(smax[:, 0, hs], bG[0][:].rearrange("p (j k) -> p j k", j=REP),
                                     AX_X, ALU.max))
                signal(v.tensor_scalar(nmax[:, u % 2, 0, hs], smax[:, 0, hs], -SCALE, None, ALU.mult),
                       "nmax_ready", 2 * n + 2)

            def normalise(u, t, bank, name):
                b, half = u // HALVES, u % HALVES
                o = bank[:, 0:HU * VC].rearrange("p (h c) -> p h c", c=VC)
                done(v.reciprocal(rsum[:], o[:, :, HD]))
                dst = A[:, b * QT + t, half * HU * HD:(half + 1) * HU * HD].rearrange("p (h d) -> p h d", d=HD)
                ins = v.tensor_tensor(dst, o[:, :, 0:HD],
                                      rsum[:].rearrange("p (h d) -> p h d", d=1).broadcast_to([P, HU, HD]), ALU.mult)
                signal(ins, name, u + 1)

            def early_norm(u):
                dve.wait_ge(s["early_pv"], GU * (u + 1))
                normalise(u, 0, bD, "early_norm")

            def late_norm(u):
                dve.wait_ge(s["late_pv"], GU * (u + 1))
                normalise(u, 1, bO, "late_norm")

            t0, t1, t2 = temp["t0"], temp["t1"], temp["t2"]
            mag, sigma, tau, theta = temp["mag"], temp["sigma"], temp["tau"], temp["theta"]
            vm, vn, flag = temp["vm"], temp["vn"], temp["flag"]

            def per_head(t, n=8):
                return t[:].rearrange("p (h d) -> p h d", d=1).broadcast_to([P, HU, n])

            def guess(u):
                nt, kk = tiny["nt"][:, u % 2], tiny["kk"][:, u % 2]
                pair(*[lambda h=h: v.bn_stats(st[:, h, :], S[:, u % 2, h, 0:P]) for h in range(HU)])
                pair(lambda: v.tensor_tensor(t0[:], st[:, :, 1], st[:, :, 4], ALU.add),
                     lambda: v.tensor_tensor(t1[:], st[:, :, 1], st[:, :, 4], ALU.subtract),
                     lambda: v.tensor_tensor(t2[:], st[:, :, 2], st[:, :, 5], ALU.add))
                done(v.tensor_tensor(t1[:], t1[:], t1[:], ALU.mult))
                done(v.scalar_tensor_tensor(out=t1[:], in0=t1[:], scalar=P / 4.0, in1=t2[:], op0=ALU.mult, op1=ALU.add))
                done(v.tensor_scalar(t1[:], t1[:], 1.0 / P, None, ALU.mult))
                done(v.tensor_scalar(t2[:].bitcast(I32), t1[:].bitcast(I32), 0.5, SQRT_BITS, ALU.mult, ALU.add))
                pair(lambda: v.tensor_scalar(kk, t2[:], k_unit, None, ALU.mult),
                     lambda: v.tensor_scalar(t2[:], t2[:], z_neg, None, ALU.mult))
                signal(v.scalar_tensor_tensor(out=nt, in0=t0[:], scalar=-0.5, in1=t2[:], op0=ALU.mult, op1=ALU.add),
                       "guess_ready", u + 1)

            def adjust(u, p):
                nt, kk, sg = tiny["nt"][:, u % 2], tiny["kk"][:, u % 2], tiny["sg"][:, u % 2]
                old, size = tiny["sg_old"][:, u % 2], tiny["size"][:, u % 2]
                dve.wait_ge(s["counted"], HU * (COUNTS * u + p + 1))
                if p == 1:
                    done(v.tensor_tensor(t0[:], old, sg, ALU.subtract))
                    done(v.scalar_tensor_tensor(out=t0[:], in0=t0[:], scalar=-1.0, in1=t0[:], op0=ALU.mult, op1=ALU.max))
                    done(v.tensor_scalar(t0[:], t0[:], 2.0, None, ALU.add))
                    done(v.reciprocal(t1[:], t0[:]))
                    done(v.scalar_tensor_tensor(out=t1[:], in0=size, scalar=2.0, in1=t1[:], op0=ALU.add, op1=ALU.mult))
                    done(v.tensor_tensor(kk, kk, t1[:], ALU.mult))
                pair(lambda: v.scalar_tensor_tensor(out=size, in0=sg, scalar=-1.0, in1=sg, op0=ALU.mult, op1=ALU.max),
                     lambda: v.tensor_tensor(t1[:], sg, kk, ALU.mult),
                     lambda: v.tensor_copy(old, sg))
                done(v.scalar_tensor_tensor(out=t2[:], in0=size, scalar=2.0 * SLACK, in1=t1[:], op0=ALU.is_gt,
                                            op1=ALU.mult))
                signal(v.tensor_tensor(nt, nt, t2[:], ALU.subtract), "adjusted", (COUNTS - 1) * u + p + 1)

            def aim(u):
                nt, sg, size = tiny["nt"][:, u % 2], tiny["sg"][:, u % 2], tiny["size"][:, u % 2]
                dve.wait_ge(s["counted"], HU * COUNTS * (u + 1))
                pair(lambda: v.tensor_scalar(t0[:], sg, 0.5, 0.5, ALU.mult, ALU.add),
                     lambda: v.tensor_scalar(t1[:], sg, 0.0, 2.0, ALU.is_lt, ALU.mult),
                     lambda: v.scalar_tensor_tensor(out=size, in0=sg, scalar=-1.0, in1=sg, op0=ALU.mult, op1=ALU.max))
                pair(lambda: v.scalar_tensor_tensor(out=mag[:], in0=t0[:], scalar=-1.0, in1=t0[:], op0=ALU.mult,
                                                    op1=ALU.max),
                     lambda: v.tensor_scalar(sigma[:], t1[:], -1.0, None, ALU.add))
                signal(v.scalar_tensor_tensor(out=tau[:], in0=sigma[:], scalar=-1.0, in1=nt, op0=ALU.mult, op1=ALU.mult),
                       "aimed", u + 1)

            def eight(u, h):
                n = u * HU + h

                def top(h):
                    v.max(V[:, h, :], W[:, (u * HU + h) % 3, :]).then_inc(s["top_made"], 1)

                dve.wait_ge(s["z_made"], n + 1)
                if n >= 3:
                    dve.wait_ge(s["top_made"], n - 2)
                z = Z[:, h % 4, :]
                v.scalar_tensor_tensor(out=W[:, n % 3, :], in0=z, scalar=tau[:, h:h + 1], in1=z, op0=ALU.is_gt,
                                       op1=ALU.subtract, reverse1=True).then_inc(s["w_made"], 1)
                if h >= 1:
                    dve.wait_ge(s["w_made"], n)
                    top(h - 1)
                if h == HU - 1:
                    dve.wait_ge(s["w_made"], n + 1)
                    top(h)

            def pick(u):
                dve.wait_ge(s["top_made"], HU * (u + 1))
                size = tiny["size"][:, u % 2]
                place = places.rearrange("p (a e) -> p a e", a=1).broadcast_to([P, HU, 8])
                pair(lambda: v.tensor_tensor(hot[:], place, per_head(mag), ALU.is_equal),
                     lambda: v.tensor_tensor(t0[:], mag[:], sigma[:], ALU.add),
                     lambda: v.tensor_tensor(flag[:], V[:, :, 0], tau[:], ALU.is_equal))
                pair(lambda: v.tensor_tensor(hot[:], hot[:], V[:], ALU.mult),
                     lambda: v.tensor_tensor(hot2[:], place, per_head(t0), ALU.is_equal))
                pair(lambda: v.tensor_reduce(vm[:], hot[:], AX_X, ALU.add),
                     lambda: v.tensor_tensor(hot2[:], hot2[:], V[:], ALU.mult),
                     lambda: v.scalar_tensor_tensor(out=t1[:], in0=size, scalar=2.0 * SLACK, in1=flag[:], op0=ALU.is_gt,
                                                    op1=ALU.max))
                pair(lambda: v.tensor_reduce(vn[:], hot2[:], AX_X, ALU.add),
                     lambda: v.tensor_tensor(theta[:], sigma[:], vm[:], ALU.mult))
                done(v.tensor_tensor(t2[:], vm[:], vn[:], ALU.is_equal))
                signal(v.tensor_tensor(flag[:], t1[:], t2[:], ALU.max), "flag_ready", u + 1)

            def keep(u):
                dve.wait_ge(s["late_exp"], HU * (u + 1))
                dve.wait_ge(s["flag_summed"], u + 1)
                pair(lambda: v.tensor_copy(flag_row[0:1, 0:HU], bO[0:1, 0:HU]),
                     lambda: v.tensor_reduce(flag_sum[0:1, :], bO[0:1, 0:HU], AX_X, ALU.add))
                done(v.tensor_copy(flag_any[0:1, :], flag_sum[0:1, :]))
                flagged = dve.value_load(flag_any[0:1, :])
                with dve.If(flagged > 0):
                    with dve.Fori(0, HU) as h:
                        rows = dve.value_load(flag_row[0:1, bass.ds(h, 1)])
                        with dve.If(rows > 0):
                            head = S[:, u % 2, bass.ds(h, 1), :]
                            v.tensor_copy(plain[:], head)
                            dve.drain()
                            v.max(m8[:], plain[:, 0])
                            dve.drain()
                            v.match_replace(taken[:, 0], m8[:], plain[:, 0], TAKEN)
                            dve.drain()
                            with dve.Fori(0, ROUNDS - 1) as _:
                                v.max(m8[:], taken[:, 0])
                                dve.drain()
                                v.match_replace(taken[:, 0], m8[:], taken[:, 0], TAKEN)
                                dve.drain()
                            v.tensor_tensor(head, taken[:], plain[:], ALU.not_equal)
                            v.tensor_scalar(theta[:, bass.ds(h, 1)], theta[:, bass.ds(h, 1)], 0.0, 0.5, ALU.mult,
                                            ALU.add)
                            dve.drain()

            def keep_group(u, g):
                for h in range(g * REP, (g + 1) * REP):
                    v.scalar_tensor_tensor(out=E[:, h, :], in0=S[:, u % 2, h, :], scalar=theta[:, h:h + 1],
                                           in1=E[:, h, :], op0=ALU.is_ge, op1=ALU.mult).then_inc(s["late_prob"], 1)
                dve.wait_ge(s["late_prob"], HU * u + (g + 1) * REP)

            def norm_scale():
                done(v.tensor_scalar(var[:], mv[:, :, 1], EPS, None, ALU.add))
                done(v.tensor_scalar(rstd[:].bitcast(I32), var[:].bitcast(I32), -0.5, RSQRT_BITS, ALU.mult, ALU.add))
                for _ in range(3):
                    done(v.tensor_tensor(sq[:], rstd[:], rstd[:], ALU.mult))
                    done(v.scalar_tensor_tensor(out=sq[:], in0=sq[:], scalar=-0.5, in1=var[:], op0=ALU.mult, op1=ALU.mult))
                    done(v.scalar_tensor_tensor(out=rstd[:], in0=sq[:], scalar=1.5, in1=rstd[:], op0=ALU.add,
                                                op1=ALU.mult))

            def layer_norm():
                pair(*[lambda t=t: v.bn_stats(st6[:, t, :], r1[:, t, :]) for t in range(QT)])
                pair(*[lambda t=t: v.bn_aggr(mv[:, t, :], st6[:, t, :]) for t in range(QT)])
                norm_scale()

            def normed(t):
                return v.tensor_scalar(x1[:, t, :], r1[:, t, :], mv[:, t, 0:1], rstd[:, t:t + 1],
                                       ALU.subtract, ALU.mult)

            def out_project(b):
                if b == 0:
                    dve.wait_ge(s["in_tok"], 32)
                for t in range(QT):
                    dve.wait_ge(s["out_ready"], b * QT + t + 1)
                    done(v.tensor_tensor(r1[:, t, :], bG[t][:], x_sb[:, b * QT + t, :], ALU.add))

            def norm_quantise(b):
                if b >= 1:
                    dve.wait_ge(s["out_done"], 16 * b)
                layer_norm()
                pair(*[lambda t=t: normed(t) for t in range(QT)])
                both = slice(0, QT)
                done(v.tensor_scalar(r1[:, both], x1[:, both], inv[:, 0:1], sc[:, 1:2], ALU.mult, ALU.add))
                done(v.tensor_scalar(r1[:, both], r1[:, both], 0.0, QMAX, ALU.max, ALU.min))
                done(v.tensor_scalar(r1[:, both], r1[:, both], MAGIC, None, ALU.add))
                for t in range(QT):
                    v.tensor_scalar(aq[:, t, :], r1[:, t, :], -(MAGIC + QMID), None, ALU.add, ALU.add,
                                    accum_out=arow[:, t:t + 1]).then_inc(s["quant_ready"], 1)
                dve.wait_ge(s["quant_ready"], QT * (b + 1))
                done(v.tensor_scalar(arow[:], arow[:], zc[:, 1:2], None, ALU.mult))

            def cross_product(b):
                dve.wait_ge(s["cadd_ready"], b + 1)
                for t in range(QT):
                    dve.wait_ge(s["cross_ready"], b * QT + t + 1)
                    done(v.scalar_tensor_tensor(out=r1[:, t, :], in0=bG[t][:], scalar=arow[:, t:t + 1],
                                                in1=cadd[:, b, :], op0=ALU.add, op1=ALU.add))
                pair(*[lambda t=t: v.scalar_tensor_tensor(out=r1[:, t, :], in0=r1[:, t, :], scalar=zc[:, 3:4],
                                                          in1=x1[:, t, :], op0=ALU.mult, op1=ALU.add)
                       for t in range(QT)])

            def norm_turn(b):
                layer_norm()
                for t in range(QT):
                    normed(t).then_inc(s["norm_ready"], 1)
                dve.wait_ge(s["norm_ready"], QT * (b + 1))

            gate_bank = ((bG[0], bG[0]), (bG[0], bS[0]))

            def hidden(b, f):
                n = b * NF + f
                bank = gate_bank[b][f % 2]
                dve.wait_ge(s["gate_done"], n + 1)
                done(v.scalar_tensor_tensor(out=g_sb[:, f % 2, :], in0=g_sb[:, f % 2, :], scalar=1.0,
                                            in1=bank[:, 0:SEQ], op0=ALU.add, op1=ALU.mult))
                signal(v.scalar_tensor_tensor(out=hT[:, f, :], in0=g_sb[:, f % 2, :], scalar=both_half[:, f:f + 1],
                                              in1=bank[:, SEQ:2 * SEQ], op0=ALU.mult, op1=ALU.mult), "h_ready", n + 1)

            def finish(b):
                dve.wait_ge(s["ff_used"], NF * (b + 1))
                for t, bank in enumerate((bD, bG[1])):
                    v.tensor_tensor(r1[:, t, :], bank[:], ds[:], ALU.mult).then_inc(s["down_used"], 1)
                dve.wait_ge(s["down_used"], QT * (b + 1))
                pair(*[lambda t=t: v.tensor_tensor(r1[:, t, :], r1[:, t, :], x1[:, t, :], ALU.add) for t in range(QT)])
                layer_norm()
                for t in range(QT):
                    normed(t).then_inc(s["y_ready"], 1)
                dve.wait_ge(s["y_ready"], QT * (b + 1))

            dve.wait_ge(s["in_cst"], 48)
            signal(v.tensor_copy(identb[:], cst[:, 0:P]), "cst_ready", 1)
            signal(v.tensor_copy(causal[:], cst[:, P:2 * P]), "cst_ready", 2)
            signal(v.memset(onesb[:], 1.0), "cst_ready", 3)
            signal(v.memset(onesf[:], 1.0), "cst_ready", 4)
            done(v.memset(vaug[:], 1.0))
            done(v.reciprocal(inv[:], sc[:]))
            done(v.tensor_scalar(zc[:, 0:1], sc[:, 1:2], QMID, -1.0, ALU.subtract, ALU.mult))
            done(v.tensor_scalar(zc[:, 1:2], sc[:, 3:4], QMID, -1.0, ALU.subtract, ALU.mult))
            done(v.tensor_tensor(zc[:, 2:3], zc[:, 0:1], zc[:, 1:2], ALU.mult))
            done(v.tensor_scalar(zc[:, 2:3], zc[:, 2:3], float(D), None, ALU.mult))
            signal(v.tensor_tensor(zc[:, 3:4], sc[:, 0:1], sc[:, 2:3], ALU.mult), "scale_ready", 1)
            dve.wait_ge(s["in_gus"], 16)
            done(v.tensor_scalar(gate_half[:], gus_sb[:, 0, :], 0.5, None, ALU.mult))
            done(v.tensor_tensor(both_half[:], gate_half[:], gus_sb[:, 1, :], ALU.mult))
            walk({"project": project, "take": take, "early_norm": early_norm, "guess": guess, "adjust": adjust,
                  "aim": aim, "eight": eight, "pick": pick, "keep": keep, "keep_group": keep_group, "late_norm": late_norm,
                  "out_project": out_project, "norm_quantise": norm_quantise, "cross_product": cross_product,
                  "norm_turn": norm_turn, "hidden": hidden, "finish": finish})



def normal_quantile(p):
    lo, hi = -8.0, 8.0
    for _ in range(60):
        mid = (lo + hi) / 2
        lo, hi = (mid, hi) if (1 + math.erf(mid / math.sqrt(2))) / 2 < p else (lo, mid)
    return (lo + hi) / 2


def kernel(**inputs):
    import concourse.bacc as bacc
    from concourse.bass_utils import run_bass_kernel_spmd

    a = {k: np.asarray(v) for k, v in inputs.items()}

    freq = 1.0 / np.float32(THETA) ** (np.arange(0, HD, 2, dtype=np.float32) / np.float32(HD))
    ang = np.outer(np.arange(SEQ, dtype=np.float32), freq).astype(np.float32)
    ang = np.concatenate([ang, ang], axis=-1)
    sign = np.concatenate([-np.ones(HD // 2), np.ones(HD // 2)]).astype(np.float32)
    table = np.stack([np.cos(ang), np.sin(ang) * sign], axis=1).astype(np.float32)
    rope = np.stack([table * np.float32(SHRINK), table], axis=1)
    causal = np.triu(np.full((P, P), MASKED, np.float32), 1)
    seen = [P + 1 + r for r in range(P)]
    z = [normal_quantile(1 - KEEP / n) for n in seen]
    z_neg = np.array([[-q] for q in z], np.float32)
    k_unit = np.array([[BOLD / (2 * n * math.exp(-q * q / 2) / math.sqrt(2 * math.pi))] for n, q in zip(seen, z)],
                      np.float32)
    places = np.broadcast_to(np.arange(8, dtype=np.float32) + np.float32(0.5), (P, 8))
    consts = np.concatenate([np.eye(P, dtype=np.float32), causal, z_neg, k_unit, places,
                             np.zeros((P, 6), np.float32)], axis=1)

    def hidden_columns(w):
        padded = np.zeros((NF * P, D), w.dtype)
        padded[:DFF] = w
        return padded.reshape(NF, P, KD, P).transpose(0, 3, 2, 1).reshape(NF, P, D)

    down = np.zeros((NF * P, D), a["L0_ffn_down_w"].dtype)
    down[:DFF] = a["L0_ffn_down_w"].T
    ffw = np.concatenate([hidden_columns(a["L0_ffn_gate_w"]), hidden_columns(a["L0_ffn_up_w"]),
                          down.reshape(NF, P, D)], axis=2)
    gus = np.zeros((2, NF * P), np.float32)
    gus[0, :DFF], gus[1, :DFF] = a["L0_ffn_gate_s"], a["L0_ffn_up_s"]
    arrays = {
        "x": a["x"],
        "xT": a["x"].reshape(B * SEQ, D).T,
        "ctx": a["ctx_4096"],
        "wqkvT": np.concatenate([a["L0_attn_Wq"], a["L0_attn_Wk"], a["L0_attn_Wv"]], axis=0).T,
        "woT": a["L0_attn_Wo"].T,
        "scal": np.concatenate([a["L0_xattn_x1_scale"], a["L0_xattn_x1_zp"],
                                a["L0_xattn_x2_scale"], a["L0_xattn_x2_zp"]]),
        "ffw": ffw,
        "gus": gus.reshape(2, NF, P).transpose(2, 0, 1),
        "down_s": a["L0_ffn_down_s"],
        "rope": rope,
        "consts": consts,
    }
    arrays = {k: np.ascontiguousarray(w) for k, w in arrays.items()}
    nc = bacc.Bacc("TRN2", target_bir_lowering=False, num_devices=1)
    args = [nc.dram_tensor(k, w.shape, mybir.dt.from_np(w.dtype), kind="ExternalInput").ap() for k, w in arrays.items()]
    out = nc.dram_tensor("out", (B, SEQ, D), F32, kind="ExternalOutput").ap()
    decoder_layer(nc, *args, out)
    result = run_bass_kernel_spmd(nc, [arrays], core_ids=[0])
    return result.results[0]["out"]
```

```python
from contextlib import ExitStack
import math

import concourse.bass as bass
from concourse import mybir
import numpy as np

P = 128
B, SEQ, D = 2, 256, 512
H, HKV, HD = 32, 8, 16
REP = H // HKV
DKV = HKV * HD
DFF = 1376
KD = D // P
NF = -(-DFF // P)
QT = SEQ // P
NQK = H + HKV
NSLOT = P // HD
NSLOTS = 4
NQ_SLOT = 5
NPART = 3
KEEP = 128
ROUNDS = KEEP // 8
HALVES = 2
HU = H // HALVES
NU = B * HALVES
GU = HU // REP
VC = HD + 1
NR = 3
PASSES = ((0, 1, 2), (3,))
NT = max(len(p) for p in PASSES)
TILES = (tuple(range(NF)), tuple(reversed(range(NF))))
THETA = 10000.0
SHRINK = 2.0 ** -40
SCALE = 0.25 / SHRINK
MASKED = -0.5
TAKEN = -1.0
COUNTS = 3
SLACK = 7
BOLD = 1.1
SQRT_BITS = 532487669.0
RSQRT_BITS = float(0x5F3759DF)
MAGIC = float(2 ** 23)
QMID = 128.0
QMAX = 255.0
EPS = 1e-5

F32, BF16, I32 = mybir.dt.float32, mybir.dt.bfloat16, mybir.dt.int32
ALU = mybir.AluOpType
ACT = mybir.ActivationFunctionType
AX_X = mybir.AxisListType.X



def further_layers(q):
    n = len(PASSES[q])
    steps = [("out_turn", q, i) for i in range(n)]
    for i in range(n):
        steps += [("out_project", q, i)] + [("out_add", q, i - 1)] * (i > 0)
    steps += [("out_add", q, n - 1), ("first_norm", q)]
    for i in range(n):
        steps += [("quantise", q, i), ("cross_turn", q, i)]
    for i in range(n):
        steps += [("cross_product", q, i)] + [("cross_add", q, i - 1)] * (i > 0)
    steps += [("cross_add", q, n - 1), ("second_norm", q)] + [("norm_turn", q, i) for i in range(n)]
    return steps


def feed_forward(q):
    steps = []
    for f in range(NF):
        steps += [("gate_up", q, f)] + [("down", q, f - 1)] * (f > 0) + [("gated", q, f)]
    return steps + [("down", q, NF - 1), ("take_down", q)]


EIGHT_FILL = {3: 4, 15: 3}
GROUP_FILL = {0: (0, 0, 0, 0), 1: (0, 0, 0, 0), 2: (2,3,0,3), 3: (0,3,0,3)}
TAIL_FILL = {"out_turn": 3, "out_project": 3, "quantise": 2, "cross_product": 3, "second_norm": 3}


def schedule():
    out, post = [], []
    groups = range(GU)

    def add(*steps):
        out.extend(steps)

    def fill(n):
        for _ in range(min(n, len(post))):
            out.append(post.pop(0))

    def counts(u, p, gs):
        add(*[("count", u, p, g) for g in gs])

    def scored(u, g):
        add(("take", u, g))
        if g < GU - 1:
            add(("scores", u, g + 1))
        if g >= 1:
            add(("early_values", u, g - 1))
        if g == GU - 1:
            add(("guess", u))
        add(("early_turn", u, g))
        if g == GU - 1:
            add(("early_values", u, g))

    add(("quantise_context", 0), ("quantise_context", 1), ("multiply", 0), ("rotate", 0), ("slots", 0), ("multiply", 1), ("rotate", 1), ("heads", 0), ("multiply", 2),
        ("slots", 1), ("heads", 1), ("rotate", 2), ("slots", 2), ("scores", 0, 0))
    for g in groups:
        scored(0, g)
    add(("scores", 1, 0), ("early_norm", 0))
    for g in range(GU - 1):
        counts(0, g, groups)
        scored(1, g)
        if g < COUNTS - 1:
            add(("adjust", 0, g))
    norms = []
    for u in range(NU):
        nxt, more = u + 1 < NU, u + 2 < NU
        add(("aim", u))
        if u == 1:
            counts(u + 1, 0, groups)
        if more:
            for g in groups:
                add(("late_exp", u, g))
        for h in range(HU):
            add(("eight", u, h))
            if h == 3:
                add(*norms)
                if u == 1:
                    add(("scores", u + 2, 0))
                if u == HALVES:
                    post = further_layers(0) + feed_forward(0)
            if u == 0 and h == 7:
                scored(1, GU - 1)
                add(("early_norm", 1), ("multiply", 3), ("heads", 2))
                counts(1, 0, groups)
            if u == 0 and h == 11:
                add(("rotate", 3), ("slots", 3), ("heads", 3), ("context", 0), ("context", 1), ("weights", 0),
                    ("scores", 2, 0))
            if not more and 4 <= h < 8:
                add(("late_exp", u, h - 4))
            if u == 2 and 4 <= h < 8:
                counts(u + 1, 0, [h - 4])
            if u == 2 and h == 8:
                add(("adjust", u + 1, 0))
            if u == 2 and 8 <= h < 12:
                counts(u + 1, 1, [h - 8])
            if u == 2:
                fill(2)
            if u == 3:
                fill(EIGHT_FILL.get(h, 0))
            if more and h == HU - 4:
                add(("adjust", u + 1, 0))
                counts(u + 1, 1, groups)
        add(("pick", u), ("keep", u))
        if u == 2:
            add(("adjust", u + 1, 1))
        for g in groups:
            add(("keep_group", u, g))
            if g >= 1:
                add(("late_values", u, g - 1))
            add(("late_turn", u, g))
            if more:
                scored(u + 2, g)
            if more and g == 0:
                add(("adjust", u + 1, 1))
            if nxt:
                counts(u + 1, 2, [g])
            fill(GROUP_FILL[u][g])
        add(("late_values", u, GU - 1))
        norms = [("early_norm", u + 2)] * more + [("late_norm", u)]
        if u == 2:
            add(("weights", 1))
    add(*norms, ("weights", 2))
    for step in further_layers(1):
        add(step)
        if step[0] in TAIL_FILL:
            fill(TAIL_FILL[step[0]])
    fill(len(post))
    end = [("final_add", 0, i) for i in range(len(PASSES[0]))] + [("final_stats", 0)]
    end += [("final_norm", 0, i) for i in range(len(PASSES[0]))]
    for step in feed_forward(1):
        add(step)
        if step[0] == "gated" and end:
            add(end.pop(0))
    add(("final_add", 1, 0), ("final_stats", 1), ("final_norm", 1, 0))
    return out


def decoder_layer(nc, x, xT, ctx, wqkvT, woT, scal, ffw, gus, down_s, rope, consts, out):
    steps_in_order = schedule()

    with ExitStack() as stack:
        def sb(name, shape, dt=F32):
            return stack.enter_context(nc.sbuf_tensor(name, shape, dt))

        def ps(name, shape, dt=F32):
            return stack.enter_context(nc.psum_tensor(name, shape, dt))

        def sem(name):
            return stack.enter_context(nc.semaphore(name))

        x_sb = sb("x_sb", [P, B * QT, D])
        front = sb("front", [P, KD * (B * SEQ + D + 2 * DKV)])
        xT_sb = front[:, 0:KD * B * SEQ].rearrange("p (k t) -> p k t", k=KD)
        wqkv = front[:, KD * B * SEQ:].rearrange("p (k n) -> p k n", k=KD)
        wo = sb("wo", [P, KD, D])
        ctx_q = sb("ctx_q", [P, B, KD, D], BF16)
        gus_sb = sb("gus_sb", [P, 2, NF])
        gate_half = sb("gate_half", [P, NF])
        both_half = sb("both_half", [P, NF])
        ds = sb("ds", [P, D])
        sc = sb("sc", [P, 4])
        inv = sb("inv", [P, 4])
        zc = sb("zc", [P, 4])
        rope_sb = sb("rope_sb", [P, QT, 2, 2, HD])
        cst = sb("cst", [P, 2 * P + 16])
        identf = cst[:, 0:P]
        z_neg, k_unit = cst[:, 2 * P:2 * P + 1], cst[:, 2 * P + 1:2 * P + 2]
        places = cst[:, 2 * P + 2:2 * P + 10]
        identb = sb("identb", [P, P], BF16)
        causal = sb("causal", [P, P], BF16)
        onesb = sb("onesb", [P, P], BF16)
        onesf = sb("onesf", [P, 1])
        TOK = NT * P
        ALL = B * QT * P
        middle = sb("middle", [P, (NF + 2) * TOK])
        q_end = NQ_SLOT * H * HD // 2
        k_end = q_end + NSLOT * DKV // 2
        r_end = 2 * k_end + NQK * HD
        q_parts_of = [middle[:, i * k_end:i * k_end + q_end].bitcast(BF16).rearrange(
            "p (h s d) -> p h s d", h=H, s=NQ_SLOT) for i in range(2)]
        k_slots_of = [middle[:, i * k_end + q_end:(i + 1) * k_end].bitcast(BF16).rearrange(
            "p (h s d) -> p h s d", h=HKV, s=NSLOT) for i in range(2)]
        rot = middle[:, 2 * k_end:r_end].rearrange("p (h d) -> p h d", h=NQK)
        rot2 = middle[:, r_end:r_end + NQK * HD].rearrange("p (h d) -> p h d", h=NQK)
        k_parts_of = sb("k_parts", [P, 2, HKV, NPART, HD], BF16)
        hT = middle[:, 0:NF * TOK].rearrange("p (f t) -> p f t", f=NF)
        g_sb = middle[:, NF * TOK:].rearrange("p (a t) -> p a t", a=2)
        qst = sb("qst", [P, NQK, SEQ], BF16)
        vaug = sb("vaug", [P, B, QT, HKV, VC])
        S = sb("S", [P, 2, HU, SEQ])
        E = sb("E", [P, HU, SEQ])
        EL = sb("EL", [P, HU, P])
        Z = sb("Z", [P, 4, SEQ])
        W = sb("W", [P, 3, SEQ])
        m8 = sb("m8", [P, 8])
        plain = sb("plain", [P, 1, SEQ])
        taken = sb("taken", [P, 1, SEQ])
        V = sb("V", [P, HU, 8])
        hot = sb("hot", [P, HU, 8])
        hot2 = sb("hot2", [P, HU, 8])
        st = sb("st", [P, HU, 6])
        smax = sb("smax", [P, QT, HU])
        nmax = sb("nmax", [P, 2, QT, HU])
        tiny = {n: sb(n, [P, 2, HU]) for n in ("nt", "kk", "sg", "sg_old", "size")}
        temp = {n: sb(n, [P, HU]) for n in ("t0", "t1", "t2", "mag", "sigma", "tau", "theta", "vm", "vn", "flag")}
        flag_row = sb("flag_row", [P, 2 * HU], I32)
        flag_sum = sb("flag_sum", [P, 1])
        flag_any = sb("flag_any", [P, 1], I32)
        ptL = sb("ptL", [P, REP, P])
        ptU = sb("ptU", [P, 2, REP, QT, P])
        rsum = sb("rsum", [P, HU])
        A = sb("A", [P, B * QT, D])
        junk = sb("junk", [P, 4, SEQ], BF16)
        spare = (S[:, 0], S[:, 1], E[:])
        ff = [front[:, i * 3 * D:(i + 1) * 3 * D] for i in range(NR)]
        ff += [m.rearrange("p h k -> p (h k)")[:, i * 3 * D:(i + 1) * 3 * D] for m in spare for i in range(2)]
        NX = len(ff) - NR

        def buffer(q, f):
            if q == 0 or f < NR:
                return TILES[q][f] % NR
            return f if f - NR < NX else buffer(1, f - NR - NX)

        xt2 = sb("xt2", [P, KD, ALL])
        r1, x1 = x_sb, A
        aq = sb("aq", [P, B * QT, D], BF16)
        aqT = sb("aqT", [P, KD, ALL], BF16)
        cadd = sb("cadd", [P, B, D])
        arow = sb("arow", [P, B * QT])
        st6 = sb("st6", [P, B * QT, 6])
        mv = sb("mv", [P, B * QT, 2])
        var = sb("var", [P, B * QT])
        rstd = sb("rstd", [P, B * QT])
        sq = sb("sq", [P, B * QT])

        bS = [ps("bS0", [P, 512]), ps("bS1", [P, 512])]
        bT = [ps("bT0", [P, 512]), ps("bT1", [P, 512])]
        bO = ps("bO", [P, 512])
        bG = [ps("bG0", [P, 512]), ps("bG1", [P, 512])]
        bD = ps("bD", [P, 512])

        names = """scale_ready in_gus in_x in_cst in_ctx in_tok in_wo cst_ready
            dve act qkv_ready qkv_used parts_ready slots_ready heads_ready heads_copied
            late_ready late_used early_ready nmax_ready late_exp early_exp late_prob
            early_turned early_copied early_pv early_norm late_turned late_copied late_pv late_norm
            guess_ready counted adjusted aimed z_made w_made top_made flag_ready flag_summed
            a_turned out_copied out_ready quant_ready cross_turned cross_copied cross_ready
            colsum_ready cadd_ready ctx_ready norm_ready x_turned x_copied
            gate_up_ready gate_done h_ready ff_used down_used y_ready out_done""".split()
        s = {n: sem(n) for n in names}
        in_w = [sem(f"in_w{k}") for k in range(KD)]
        in_ff = [sem(f"in_ff{i}") for i in range(len(ff))]

        project_bank = (bG, bS, bG, bG)

        turn_bank = (bD, bG[1], bS[1], bT[0])
        product_bank = (bG[0], bS[0], bD, bT[1])

        def tokens(q):
            return slice(PASSES[q][0] * P, (PASSES[q][-1] + 1) * P)

        def gate_up(q, f):
            n = len(PASSES[q]) * P
            if q == 0:
                return bG[0][:, 0:n], bS[0][:, 0:n]
            bank = (bT[1], bO)[f % 2]
            return bank[:, 0:n], bank[:, n:2 * n]

        def walk(handlers):
            for step in steps_in_order:
                if step[0] in handlers:
                    handlers[step[0]](*step[1:])

        block = stack.enter_context(nc.Block())

        @block.sync
        def _(sp):
            x_by_part = xT.rearrange("(k p) t -> p k t", p=P)
            sp.dma_start(xT_sb[:, :, 0:P], x_by_part[:, :, 0:P]).then_inc(s["in_x"], 16)
            for k in range(KD):
                sp.dma_start(wqkv[:, k, :], wqkvT[k * P:(k + 1) * P, :]).then_inc(in_w[k], 16)
            sp.dma_start(xT_sb[:, :, P:B * SEQ], x_by_part[:, :, P:B * SEQ]).then_inc(s["in_x"], 16)
            sp.dma_start(cst[:], consts).then_inc(s["in_cst"], 16)
            sp.dma_start(rope_sb[:], rope.rearrange("(t p) a r d -> p t a r d", p=P)).then_inc(s["in_cst"], 16)
            sp.dma_start(sc[:], scal[None, :].broadcast_to([P, 4])).then_inc(s["in_cst"], 16)
            sp.dma_start(gus_sb[:], gus).then_inc(s["in_gus"], 16)
            sp.dma_start(E[:].rearrange("p (b k a) n -> p b k (a n)", b=B, k=KD),
                         ctx.rearrange("b (k p) n -> p b k n", p=P)).then_inc(s["in_ctx"], 16)
            sp.dma_start(x_sb[:], x.rearrange("b (t p) d -> p (b t) d", p=P)).then_inc(s["in_tok"], 16)
            sp.dma_start(ds[:], down_s[None, :].broadcast_to([P, D])).then_inc(s["in_tok"], 16)
            sp.dma_start(wo[:], woT.rearrange("(k p) n -> p k n", p=P)).then_inc(s["in_wo"], 16)
            for tt in range(B * QT):
                sp.wait_ge(s["y_ready"], tt + 1)
                t = tt % QT * P
                sp.dma_start(out[tt // QT, t:t + P, :], x1[:, tt, :]).then_inc(s["out_done"], 16)
            sp.wait_ge(s["out_done"], 16 * B * QT)

        @block.gpsimd
        def _(pool):
            def load(q, f):
                pool.dma_start(ff[buffer(q, f)], ffw[TILES[q][f]]).then_inc(in_ff[buffer(q, f)], 16)

            def weights(stage):
                if stage == 0:
                    pool.wait_ge(s["qkv_ready"], B * QT)
                    for f in range(NR):
                        load(0, f)
                if stage == 1:
                    pool.wait_ge(s["late_prob"], 3 * HU)
                    for f in range(NR, NR + 2):
                        load(1, f)
                if stage == 2:
                    pool.wait_ge(s["late_prob"], NU * HU)
                    pool.wait_ge(s["late_turned"], QT * NU * GU)
                    for f in range(NR + 2, NR + NX):
                        load(1, f)

            def refill(q, f):
                used = f - 2 if q == 0 else f - 1
                nxt = used + NR if q == 0 else used + NR + NX
                if used >= 0 and nxt < NF:
                    pool.wait_ge(s["ff_used"], q * NF + used + 1)
                    load(q, nxt)

            def context(b):
                if b == 0:
                    pool.wait_ge(s["in_ctx"], 16)
                    pool.wait_ge(s["scale_ready"], 1)
                c = E[:, b * HU // 2:(b + 1) * HU // 2, :].rearrange("p (k a) n -> p k (a n)", k=KD)
                base = 4 * b
                nc.gpsimd.tensor_scalar(c, c, inv[:, 2:3], sc[:, 3:4], ALU.mult, ALU.add).then_inc(s["ctx_ready"], 1)
                pool.wait_ge(s["ctx_ready"], base + 1)
                nc.gpsimd.tensor_scalar(c, c, QMAX, 0.0, ALU.min, ALU.max).then_inc(s["ctx_ready"], 1)
                pool.wait_ge(s["ctx_ready"], base + 2)
                nc.gpsimd.tensor_scalar(c, c, MAGIC, 1.0, ALU.add, ALU.mult).then_inc(s["ctx_ready"], 1)
                pool.wait_ge(s["ctx_ready"], base + 3)
                nc.gpsimd.tensor_scalar(ctx_q[:, b], c, -(MAGIC + QMID), 1.0, ALU.add,
                                        ALU.mult).then_inc(s["ctx_ready"], 1)

            def eight(u, h):
                n = u * HU + h
                if h == 0:
                    pool.wait_ge(s["aimed"], u + 1)
                if n >= 4:
                    pool.wait_ge(s["w_made"], n - 3)
                nc.gpsimd.tensor_scalar(Z[:, h % 4, :], S[:, u % 2, h, :], temp["sigma"][:, h:h + 1], 1.0,
                                        ALU.mult, ALU.mult).then_inc(s["z_made"], 1)

            walk({"weights": weights, "gate_up": refill, "quantise_context": context, "eight": eight})

        @block.tensor
        def _(pe):
            def project(tt):
                if tt == 0:
                    pe.wait_ge(s["in_x"], 16)
                if tt == 1:
                    pe.wait_ge(s["in_x"], 32)
                if tt == 2:
                    pe.wait_ge(s["qkv_used"], 1)
                if tt == 3:
                    pe.wait_ge(s["qkv_used"], 3)
                    pe.wait_ge(s["early_exp"], 2 * GU)
                    pe.wait_ge(s["early_copied"], 2 * GU)
                for dst, lo, n in ((project_bank[tt][0], 0, D), (project_bank[tt][1], D, 2 * DKV)):
                    for k in range(KD):
                        if tt == 0 and lo == 0:
                            pe.wait_ge(in_w[k], 16)
                        last = nc.tensor.matmul(dst[:, 0:n], xT_sb[:, k, tt * P:(tt + 1) * P],
                                                wqkv[:, k, lo:lo + n], start=(k == 0), stop=(k == KD - 1))
                last.then_inc(s["qkv_ready"], 1)

            def heads(tt):
                if tt == 0:
                    pe.wait_ge(s["cst_ready"], 4)
                q_parts, k_slots = q_parts_of[tt % 2], k_slots_of[tt % 2]
                pe.wait_ge(s["slots_ready"], NSLOTS * (tt + 1))
                n = NQK // 8
                for j in range(n):
                    e = tt * n + j
                    if e >= 2:
                        pe.wait_ge(s["heads_copied"], e - 1)
                    bank = bT[e % 2][:].bitcast(BF16)
                    for h in range(8):
                        if j < H // 8:
                            head = q_parts[:, 8 * j + h].rearrange("p s d -> p (s d)")
                            nc.tensor.transpose(bank[0:P // 2, h * P:(h + 1) * P], head[:, 0:4 * HD], identb[:])
                            last = nc.tensor.transpose(bank[P // 2:P, h * P:(h + 1) * P], head[:, HD:5 * HD],
                                                       identb[:])
                        else:
                            last = nc.tensor.transpose(bank[:, h * P:(h + 1) * P],
                                                       k_slots[:, h].rearrange("p s d -> p (s d)"), identb[:])
                    last.then_inc(s["heads_ready"], 1)

            def context(b):
                pe.wait_ge(s["ctx_ready"], 4 * (b + 1))
                if b == 0:
                    pe.wait_ge(s["early_norm"], HALVES)
                else:
                    pe.wait_ge(s["cadd_ready"], 1)
                for k in range(KD):
                    last = nc.tensor.matmul(bD[:], onesb[:], ctx_q[:, b, k, :], start=(k == 0), stop=(k == KD - 1))
                last.then_inc(s["colsum_ready"], 1)

            def scores(u, g):
                b, half, n = u // HALVES, u % HALVES, u * GU + g
                kk = qst[:, H + half * GU + g, :]
                if g == 0 and half == 0:
                    pe.wait_ge(s["heads_copied"], (b + 1) * QT * NQK // 8)
                if g == 0:
                    pe.wait_ge(s["qkv_used"], 2 + (b == 1) * QT)
                for pair in range(REP // 2):
                    if n >= 1:
                        pe.wait_ge(s["late_used"], (n - 1) * REP + 2 * pair + 2)
                    for j in range(2):
                        q = qst[:, half * HU + g * REP + 2 * pair + j, :]
                        nc.tensor.matmul(bS[pair][:, j * SEQ:(j + 1) * SEQ], q[:, P:SEQ], kk, start=True, stop=False,
                                         skip_group_check=True)
                        last = nc.tensor.matmul(bS[pair][:, j * SEQ + P:(j + 1) * SEQ], identb[:], causal[:],
                                                start=False, stop=True, skip_group_check=True)
                    last.then_inc(s["late_ready"], 1)
                if g == 0 and u == 0:
                    pe.wait_ge(s["qkv_used"], 3)
                if n >= 1:
                    pe.wait_ge(s["early_exp"], n)
                for j in range(REP):
                    q = qst[:, half * HU + g * REP + j, :]
                    nc.tensor.matmul(bG[0][:, j * P:(j + 1) * P], q[:, 0:P], kk[:, 0:P], start=True, stop=False,
                                     skip_group_check=True)
                    last = nc.tensor.matmul(bG[0][:, j * P:(j + 1) * P], identb[:], causal[:], start=False, stop=True,
                                            skip_group_check=True)
                last.then_inc(s["early_ready"], 1)

            def early_turn(u, g):
                n = u * GU + g
                pe.wait_ge(s["early_exp"], n + 1)
                if n >= 1:
                    pe.wait_ge(s["early_copied"], n)
                for j in range(REP):
                    last = nc.tensor.transpose(bG[1][:, j * P:(j + 1) * P], EL[:, g * REP + j, :], identf)
                last.then_inc(s["early_turned"], 1)

            def early_values(u, g):
                b, half, n = u // HALVES, u % HALVES, u * GU + g
                pe.wait_ge(s["early_copied"], n + 1)
                if g == 0 and u >= 1:
                    pe.wait_ge(s["early_norm"], u)
                if g == 0 and u == HALVES:
                    pe.wait_ge(s["cadd_ready"], B)
                for j in range(REP):
                    c = (g * REP + j) * VC
                    last = nc.tensor.matmul(bD[:, c:c + VC], ptL[:, j, :], vaug[:, b, 0, half * GU + g, :],
                                            start=True, stop=True)
                last.then_inc(s["early_pv"], 1)

            def pick(u):
                pe.wait_ge(s["flag_ready"], u + 1)
                if u >= 1:
                    pe.wait_ge(s["late_norm"], u)
                nc.tensor.matmul(bO[0:1, 0:HU], onesf[:], temp["flag"][:], start=True,
                                 stop=True).then_inc(s["flag_summed"], 1)

            def late_turn(u, g):
                n = u * GU + g
                pe.wait_ge(s["late_prob"], n * REP + REP)
                if n == 0:
                    pe.wait_ge(s["heads_copied"], B * QT * NQK // 8)
                for kt in range(QT):
                    if n >= 1:
                        pe.wait_ge(s["late_copied"], QT * (n - 1) + kt + 1)
                    for j in range(REP):
                        last = nc.tensor.transpose(bT[kt][:, j * P:(j + 1) * P],
                                                   E[:, g * REP + j, kt * P:(kt + 1) * P], identf)
                    last.then_inc(s["late_turned"], 1)

            def late_values(u, g):
                b, half, n = u // HALVES, u % HALVES, u * GU + g
                pe.wait_ge(s["late_copied"], QT * (n + 1))
                for j in range(REP):
                    c = (g * REP + j) * VC
                    for kt in range(QT):
                        last = nc.tensor.matmul(bO[:, c:c + VC], ptU[:, n % 2, j, kt, :],
                                                vaug[:, b, kt, half * GU + g, :],
                                                start=(kt == 0), stop=(kt == QT - 1))
                last.then_inc(s["late_pv"], 1)

            def turn(q, i, src, ident, name):
                tt = PASSES[q][i]
                bank = turn_bank[tt][:] if ident is identf else turn_bank[tt][:].bitcast(BF16)
                for k in range(KD):
                    last = nc.tensor.transpose(bank[:, k * P:(k + 1) * P], src[:, k * P:(k + 1) * P],
                                               ident if ident is identf else ident[:])
                last.then_inc(s[name], 1)

            def multiply(q, i, lhsT, rhs, copied, name):
                tt = PASSES[q][i]
                pe.wait_ge(s[copied], tt + 1)
                for k in range(KD):
                    last = nc.tensor.matmul(product_bank[tt][:], lhsT[:, k, tt * P:(tt + 1) * P], rhs(k),
                                            start=(k == 0), stop=(k == KD - 1))
                last.then_inc(s[name], 1)

            def out_turn(q, i):
                if q == 0 and i == 0:
                    pe.wait_ge(s["late_norm"], HALVES)
                    pe.wait_ge(s["early_norm"], NU)
                    pe.wait_ge(s["early_exp"], NU * GU)
                    pe.wait_ge(s["early_copied"], NU * GU)
                    pe.wait_ge(s["late_used"], NU * HU)
                if q == 1:
                    pe.wait_ge(s["late_norm"], NU)
                turn(q, i, A[:, PASSES[q][i], :], identf, "a_turned")

            def out_project(q, i):
                if q == 0 and i == 0:
                    pe.wait_ge(s["in_wo"], 16)
                multiply(q, i, xt2, lambda k: wo[:, k, :], "out_copied", "out_ready")

            def cross_turn(q, i):
                pe.wait_ge(s["quant_ready"], PASSES[q][i] + 1)
                turn(q, i, aq[:, PASSES[q][i], :], identb, "cross_turned")

            def cross_product(q, i):
                b = PASSES[q][i] // QT
                multiply(q, i, aqT, lambda k: ctx_q[:, b, k, :], "cross_copied", "cross_ready")

            def norm_turn(q, i):
                pe.wait_ge(s["norm_ready"], PASSES[q][i] + 1)
                turn(q, i, x1[:, PASSES[q][i], :], identf, "x_turned")

            def hidden(q, f):
                n, w = q * NF + f, buffer(q, f)
                if f == 0:
                    pe.wait_ge(s["x_copied"], PASSES[q][-1] + 1)
                if q == 0 or f >= NR:
                    past = sum(buffer(0, e) == w for e in range(NF if q else f + 1))
                    again = sum(buffer(1, e) == w for e in range(NR, f + 1)) if q else 0
                    pe.wait_ge(in_ff[w], 16 * (past + again))
                if q == 0 and f >= 1:
                    pe.wait_ge(s["h_ready"], n)
                if q == 1 and f >= 2:
                    pe.wait_ge(s["h_ready"], n - 1)
                for j, dst in enumerate(gate_up(q, f)):
                    for k in range(KD):
                        last = nc.tensor.matmul(dst, ff[w][:, j * D + k * P:j * D + (k + 1) * P], xt2[:, k, tokens(q)],
                                                start=(k == 0), stop=(k == KD - 1))
                last.then_inc(s["gate_up_ready"], 1)

            def down(q, f):
                pe.wait_ge(s["h_ready"], q * NF + f + 1)
                for i, tt in enumerate(PASSES[q]):
                    last = nc.tensor.matmul(turn_bank[tt][:], hT[:, f, i * P:(i + 1) * P],
                                            ff[buffer(q, f)][:, 2 * D:3 * D],
                                            start=(f == 0), stop=(f == NF - 1), skip_group_check=True)
                last.then_inc(s["ff_used"], 1)

            walk({"multiply": project, "heads": heads, "context": context, "scores": scores, "early_turn": early_turn,
                  "early_values": early_values, "pick": pick, "late_turn": late_turn, "late_values": late_values, "out_turn": out_turn, "out_project": out_project,
                  "cross_turn": cross_turn, "cross_product": cross_product, "norm_turn": norm_turn,
                  "gate_up": hidden, "down": down})

        @block.scalar
        def _(act):
            def slots(tt):
                q_parts, k_slots, k_parts = q_parts_of[tt % 2], k_slots_of[tt % 2], k_parts_of[:, tt % 2]
                act.wait_ge(s["parts_ready"], 2 * (tt + 1))
                nc.scalar.activation(q_parts[:, :, NPART:NQ_SLOT, :], q_parts[:, :, 0:2, :],
                                     ACT.Copy).then_inc(s["slots_ready"], 1)
                for part, lo, hi in ((0, 0, 3), (1, 3, 6), (2, 6, 8)):
                    src = k_parts[:, :, part:part + 1, :].broadcast_to([P, HKV, hi - lo, HD])
                    nc.scalar.activation(k_slots[:, :, lo:hi, :], src, ACT.Copy).then_inc(s["slots_ready"], 1)

            def heads(tt):
                t, n = tt % QT, NQK // 8
                for j in range(n):
                    e = tt * n + j
                    act.wait_ge(s["heads_ready"], e + 1)
                    nc.scalar.activation(qst[:, 8 * j:8 * j + 8, t * P:(t + 1) * P],
                                         bT[e % 2][:].bitcast(BF16).rearrange("p (h t) -> p h t", h=8),
                                         ACT.Copy).then_inc(s["heads_copied"], 1)

            def context(b):
                act.wait_ge(s["colsum_ready"], b + 1)
                nc.scalar.activation(cadd[:, b, :], bD[:], ACT.Identity, bias=zc[:, 2:3],
                                     scale=zc[:, 0:1]).then_inc(s["cadd_ready"], 1)

            def take(u, g):
                n = u * GU + g
                act.wait_ge(s["early_ready"], n + 1)
                act.wait_ge(s["nmax_ready"], 2 * n + 2)
                if u >= 1:
                    act.wait_ge(s["early_turned"], n - GU + 1)
                for j in range(REP):
                    h = g * REP + j
                    last = nc.scalar.activation(EL[:, h, :], bG[0][:, j * P:(j + 1) * P], ACT.Exp,
                                                bias=nmax[:, u % 2, 0, h:h + 1], scale=SCALE)
                last.then_inc(s["early_exp"], 1)

            def early_turn(u, g):
                n = u * GU + g
                act.wait_ge(s["early_turned"], n + 1)
                if n >= 1:
                    act.wait_ge(s["early_pv"], n)
                nc.scalar.activation(ptL[:], bG[1][:].rearrange("p (j q) -> p j q", j=REP),
                                     ACT.Copy).then_inc(s["early_copied"], 1)

            def count(u, p, g):
                if p == 0:
                    act.wait_ge(s["guess_ready"], u + 1)
                else:
                    act.wait_ge(s["adjusted"], (COUNTS - 1) * u + p)
                for h in range(g * REP, (g + 1) * REP):
                    c = (u * COUNTS + p) * HU + h
                    if c >= 4:
                        act.wait_ge(s["counted"], c - 3)
                    nc.scalar.activation(junk[:, c % 4, :], S[:, u % 2, h, :], ACT.Sign,
                                         bias=tiny["nt"][:, u % 2, h:h + 1],
                                         accum_out=tiny["sg"][:, u % 2, h:h + 1]).then_inc(s["counted"], 1)

            def late_exp(u, g):
                for h in range(g * REP, (g + 1) * REP):
                    if u == 0 and h == 0:
                        act.wait_ge(s["ctx_ready"], 4 * B)
                    if u >= 1 and h % REP == 0:
                        act.wait_ge(s["late_turned"], QT * ((u - 1) * GU + h // REP + 1))
                    nc.scalar.activation(E[:, h, :], S[:, u % 2, h, :], ACT.Exp, bias=nmax[:, u % 2, 1, h:h + 1],
                                         scale=SCALE).then_inc(s["late_exp"], 1)

            def late_turn(u, g):
                n = u * GU + g
                for kt in range(QT):
                    act.wait_ge(s["late_turned"], QT * n + kt + 1)
                    if n >= 2:
                        act.wait_ge(s["late_pv"], n - 1)
                    nc.scalar.activation(ptU[:, n % 2, :, kt, :], bT[kt][:].rearrange("p (j q) -> p j q", j=REP),
                                         ACT.Copy).then_inc(s["late_copied"], 1)

            def copy(q, i, dst, turned, copied):
                act.wait_ge(s[turned], PASSES[q][i] + 1)
                tt = PASSES[q][i]
                src = turn_bank[tt][:] if dst is xt2 else turn_bank[tt][:].bitcast(BF16)[:, 0:D]
                nc.scalar.activation(dst[:, :, tt * P:(tt + 1) * P], src.rearrange("p (k q) -> p k q", k=KD),
                                     ACT.Copy).then_inc(s[copied], 1)

            def out_turn(q, i):
                copy(q, i, xt2, "a_turned", "out_copied")

            def cross_turn(q, i):
                copy(q, i, aqT, "cross_turned", "cross_copied")

            def norm_turn(q, i):
                copy(q, i, xt2, "x_turned", "x_copied")

            def gated(q, f):
                n, toks, w = q * NF + f, len(PASSES[q]) * P, TILES[q][f]
                act.wait_ge(s["gate_up_ready"], n + 1)
                if n >= 2:
                    act.wait_ge(s["h_ready"], n - 1)
                nc.scalar.activation(g_sb[:, f % 2, 0:toks], gate_up(q, f)[0], ACT.Tanh,
                                     scale=gate_half[:, w:w + 1]).then_inc(s["gate_done"], 1)

            act.wait_ge(s["scale_ready"], 1)
            walk({"slots": slots, "heads": heads, "context": context, "take": take, "early_turn": early_turn,
                  "count": count, "late_exp": late_exp, "late_turn": late_turn, "out_turn": out_turn,
                  "cross_turn": cross_turn, "norm_turn": norm_turn, "gated": gated})

        @block.vector
        def _(dve):
            steps = [0]
            v = nc.vector

            def done(ins):
                steps[0] += 1
                ins.then_inc(s["dve"], 1)
                dve.wait_ge(s["dve"], steps[0])

            def pair(*instructions):
                for ins in instructions:
                    steps[0] += 1
                    ins().then_inc(s["dve"], 1)
                dve.wait_ge(s["dve"], steps[0])

            def signal(ins, name, count):
                ins.then_inc(s[name], 1)
                dve.wait_ge(s[name], count)

            def project(tt):
                b, t = tt // QT, tt % QT
                q_parts, k_parts = q_parts_of[tt % 2], k_parts_of[:, tt % 2]
                queries, others = project_bank[tt]
                dve.wait_ge(s["qkv_ready"], tt + 1)
                hf = HD // 2
                for a, (lo, n, src) in enumerate(((0, H, queries[:]), (H, HKV, others[:, 0:DKV]))):
                    src = src.rearrange("p (h d) -> p h d", d=HD)

                    def table(r, c0, c1):
                        return rope_sb[:, t, a, r:r + 1, c0:c1].broadcast_to([P, n, c1 - c0])

                    pair(lambda: v.tensor_tensor(rot[:, lo:lo + n, :], src, table(0, 0, HD), ALU.mult),
                         lambda: v.tensor_tensor(rot2[:, lo:lo + n, 0:hf], src[:, :, hf:HD], table(1, 0, hf), ALU.mult),
                         lambda: v.tensor_tensor(rot2[:, lo:lo + n, hf:HD], src[:, :, 0:hf], table(1, hf, HD), ALU.mult))
                signal(v.tensor_copy(vaug[:, b, t, :, 0:HD], others[:, DKV:2 * DKV].rearrange("p (h d) -> p h d", d=HD)),
                       "qkv_used", tt + 1)
                done(v.tensor_tensor(rot, rot, rot2, ALU.add))
                if tt >= 2:
                    dve.wait_ge(s["heads_ready"], (tt - 1) * NQK // 8)
                heads = ((rot[:, 0:H], q_parts), (rot[:, H:NQK], k_parts))
                for part in range(NPART - 1):
                    pair(*[lambda r=r, w=w: v.tensor_copy(w[:, :, part, :], r) for r, w in heads])
                    if part == 0:
                        pair(*[lambda r=r, w=w: v.tensor_tensor(r, r, w[:, :, 0, :], ALU.subtract) for r, w in heads])
                for r, w in heads:
                    v.tensor_tensor(w[:, :, 2, :], r, w[:, :, 1, :], ALU.subtract).then_inc(s["parts_ready"], 1)
                dve.wait_ge(s["parts_ready"], 2 * (tt + 1))

            def take(u, g):
                n = u * GU + g
                hs = slice(g * REP, (g + 1) * REP)
                for j in range(REP):
                    h = g * REP + j
                    if j % 2 == 0:
                        dve.wait_ge(s["late_ready"], 2 * n + j // 2 + 1)
                    v.tensor_scalar(S[:, u % 2, h, :], bS[j // 2][:, j % 2 * SEQ:(j % 2 + 1) * SEQ], 1.0,
                                    None, ALU.mult, ALU.max, accum_out=smax[:, 1, h:h + 1]).then_inc(s["late_used"], 1)
                dve.wait_ge(s["late_used"], REP * (n + 1))
                v.tensor_scalar(nmax[:, u % 2, 1, hs], smax[:, 1, hs], -SCALE, None,
                                ALU.mult).then_inc(s["nmax_ready"], 1)
                dve.wait_ge(s["early_ready"], n + 1)
                done(v.tensor_reduce(smax[:, 0, hs], bG[0][:].rearrange("p (j k) -> p j k", j=REP),
                                     AX_X, ALU.max))
                signal(v.tensor_scalar(nmax[:, u % 2, 0, hs], smax[:, 0, hs], -SCALE, None, ALU.mult),
                       "nmax_ready", 2 * n + 2)

            def normalise(u, t, bank, name):
                b, half = u // HALVES, u % HALVES
                o = bank[:, 0:HU * VC].rearrange("p (h c) -> p h c", c=VC)
                done(v.reciprocal(rsum[:], o[:, :, HD]))
                dst = A[:, b * QT + t, half * HU * HD:(half + 1) * HU * HD].rearrange("p (h d) -> p h d", d=HD)
                ins = v.tensor_tensor(dst, o[:, :, 0:HD],
                                      rsum[:].rearrange("p (h d) -> p h d", d=1).broadcast_to([P, HU, HD]), ALU.mult)
                signal(ins, name, u + 1)

            def early_norm(u):
                dve.wait_ge(s["early_pv"], GU * (u + 1))
                normalise(u, 0, bD, "early_norm")

            def late_norm(u):
                dve.wait_ge(s["late_pv"], GU * (u + 1))
                normalise(u, 1, bO, "late_norm")

            t0, t1, t2 = temp["t0"], temp["t1"], temp["t2"]
            mag, sigma, tau, theta = temp["mag"], temp["sigma"], temp["tau"], temp["theta"]
            vm, vn, flag = temp["vm"], temp["vn"], temp["flag"]

            def per_head(t, n=8):
                return t[:].rearrange("p (h d) -> p h d", d=1).broadcast_to([P, HU, n])

            def guess(u):
                nt, kk = tiny["nt"][:, u % 2], tiny["kk"][:, u % 2]
                pair(*[lambda h=h: v.bn_stats(st[:, h, :], S[:, u % 2, h, 0:P]) for h in range(HU)])
                pair(lambda: v.tensor_tensor(t0[:], st[:, :, 1], st[:, :, 4], ALU.add),
                     lambda: v.tensor_tensor(t1[:], st[:, :, 1], st[:, :, 4], ALU.subtract),
                     lambda: v.tensor_tensor(t2[:], st[:, :, 2], st[:, :, 5], ALU.add))
                done(v.tensor_tensor(t1[:], t1[:], t1[:], ALU.mult))
                done(v.scalar_tensor_tensor(out=t1[:], in0=t1[:], scalar=P / 4.0, in1=t2[:], op0=ALU.mult, op1=ALU.add))
                done(v.tensor_scalar(t1[:], t1[:], 1.0 / P, None, ALU.mult))
                done(v.tensor_scalar(t2[:].bitcast(I32), t1[:].bitcast(I32), 0.5, SQRT_BITS, ALU.mult, ALU.add))
                pair(lambda: v.tensor_scalar(kk, t2[:], k_unit, None, ALU.mult),
                     lambda: v.tensor_scalar(t2[:], t2[:], z_neg, None, ALU.mult))
                signal(v.scalar_tensor_tensor(out=nt, in0=t0[:], scalar=-0.5, in1=t2[:], op0=ALU.mult, op1=ALU.add),
                       "guess_ready", u + 1)

            def adjust(u, p):
                nt, kk, sg = tiny["nt"][:, u % 2], tiny["kk"][:, u % 2], tiny["sg"][:, u % 2]
                old, size = tiny["sg_old"][:, u % 2], tiny["size"][:, u % 2]
                dve.wait_ge(s["counted"], HU * (COUNTS * u + p + 1))
                if p == 1:
                    done(v.tensor_tensor(t0[:], old, sg, ALU.subtract))
                    done(v.scalar_tensor_tensor(out=t0[:], in0=t0[:], scalar=-1.0, in1=t0[:], op0=ALU.mult, op1=ALU.max))
                    done(v.tensor_scalar(t0[:], t0[:], 2.0, None, ALU.add))
                    done(v.reciprocal(t1[:], t0[:]))
                    done(v.scalar_tensor_tensor(out=t1[:], in0=size, scalar=2.0, in1=t1[:], op0=ALU.add, op1=ALU.mult))
                    done(v.tensor_tensor(kk, kk, t1[:], ALU.mult))
                pair(lambda: v.scalar_tensor_tensor(out=size, in0=sg, scalar=-1.0, in1=sg, op0=ALU.mult, op1=ALU.max),
                     lambda: v.tensor_tensor(t1[:], sg, kk, ALU.mult),
                     lambda: v.tensor_copy(old, sg))
                done(v.scalar_tensor_tensor(out=t2[:], in0=size, scalar=2.0 * SLACK, in1=t1[:], op0=ALU.is_gt,
                                            op1=ALU.mult))
                signal(v.tensor_tensor(nt, nt, t2[:], ALU.subtract), "adjusted", (COUNTS - 1) * u + p + 1)

            def aim(u):
                nt, sg, size = tiny["nt"][:, u % 2], tiny["sg"][:, u % 2], tiny["size"][:, u % 2]
                dve.wait_ge(s["counted"], HU * COUNTS * (u + 1))
                pair(lambda: v.tensor_scalar(t0[:], sg, 0.5, 0.5, ALU.mult, ALU.add),
                     lambda: v.tensor_scalar(t1[:], sg, 0.0, 2.0, ALU.is_lt, ALU.mult),
                     lambda: v.scalar_tensor_tensor(out=size, in0=sg, scalar=-1.0, in1=sg, op0=ALU.mult, op1=ALU.max))
                pair(lambda: v.scalar_tensor_tensor(out=mag[:], in0=t0[:], scalar=-1.0, in1=t0[:], op0=ALU.mult,
                                                    op1=ALU.max),
                     lambda: v.tensor_scalar(sigma[:], t1[:], -1.0, None, ALU.add))
                signal(v.scalar_tensor_tensor(out=tau[:], in0=sigma[:], scalar=-1.0, in1=nt, op0=ALU.mult, op1=ALU.mult),
                       "aimed", u + 1)

            def eight(u, h):
                n = u * HU + h

                def top(h):
                    v.max(V[:, h, :], W[:, (u * HU + h) % 3, :]).then_inc(s["top_made"], 1)

                dve.wait_ge(s["z_made"], n + 1)
                if n >= 3:
                    dve.wait_ge(s["top_made"], n - 2)
                z = Z[:, h % 4, :]
                v.scalar_tensor_tensor(out=W[:, n % 3, :], in0=z, scalar=tau[:, h:h + 1], in1=z, op0=ALU.is_gt,
                                       op1=ALU.subtract, reverse1=True).then_inc(s["w_made"], 1)
                if h >= 1:
                    dve.wait_ge(s["w_made"], n)
                    top(h - 1)
                if h == HU - 1:
                    dve.wait_ge(s["w_made"], n + 1)
                    top(h)

            def pick(u):
                dve.wait_ge(s["top_made"], HU * (u + 1))
                size = tiny["size"][:, u % 2]
                place = places.rearrange("p (a e) -> p a e", a=1).broadcast_to([P, HU, 8])
                pair(lambda: v.tensor_tensor(hot[:], place, per_head(mag), ALU.is_equal),
                     lambda: v.tensor_tensor(t0[:], mag[:], sigma[:], ALU.add),
                     lambda: v.tensor_tensor(flag[:], V[:, :, 0], tau[:], ALU.is_equal))
                pair(lambda: v.tensor_tensor(hot[:], hot[:], V[:], ALU.mult),
                     lambda: v.tensor_tensor(hot2[:], place, per_head(t0), ALU.is_equal))
                pair(lambda: v.tensor_reduce(vm[:], hot[:], AX_X, ALU.add),
                     lambda: v.tensor_tensor(hot2[:], hot2[:], V[:], ALU.mult),
                     lambda: v.scalar_tensor_tensor(out=t1[:], in0=size, scalar=2.0 * SLACK, in1=flag[:], op0=ALU.is_gt,
                                                    op1=ALU.max))
                pair(lambda: v.tensor_reduce(vn[:], hot2[:], AX_X, ALU.add),
                     lambda: v.tensor_tensor(theta[:], sigma[:], vm[:], ALU.mult))
                done(v.tensor_tensor(t2[:], vm[:], vn[:], ALU.is_equal))
                signal(v.tensor_tensor(flag[:], t1[:], t2[:], ALU.max), "flag_ready", u + 1)

            def keep(u):
                dve.wait_ge(s["late_exp"], HU * (u + 1))
                dve.wait_ge(s["flag_summed"], u + 1)
                pair(lambda: v.tensor_copy(flag_row[0:1, 0:HU], bO[0:1, 0:HU]),
                     lambda: v.tensor_reduce(flag_sum[0:1, :], bO[0:1, 0:HU], AX_X, ALU.add))
                done(v.tensor_copy(flag_any[0:1, :], flag_sum[0:1, :]))
                flagged = dve.value_load(flag_any[0:1, :])
                with dve.If(flagged > 0):
                    with dve.Fori(0, HU) as h:
                        rows = dve.value_load(flag_row[0:1, bass.ds(h, 1)])
                        with dve.If(rows > 0):
                            head = S[:, u % 2, bass.ds(h, 1), :]
                            v.tensor_copy(plain[:], head)
                            dve.drain()
                            v.max(m8[:], plain[:, 0])
                            dve.drain()
                            v.match_replace(taken[:, 0], m8[:], plain[:, 0], TAKEN)
                            dve.drain()
                            with dve.Fori(0, ROUNDS - 1) as _:
                                v.max(m8[:], taken[:, 0])
                                dve.drain()
                                v.match_replace(taken[:, 0], m8[:], taken[:, 0], TAKEN)
                                dve.drain()
                            v.tensor_tensor(head, taken[:], plain[:], ALU.not_equal)
                            v.tensor_scalar(theta[:, bass.ds(h, 1)], theta[:, bass.ds(h, 1)], 0.0, 0.5, ALU.mult,
                                            ALU.add)
                            dve.drain()

            def keep_group(u, g):
                for h in range(g * REP, (g + 1) * REP):
                    v.scalar_tensor_tensor(out=E[:, h, :], in0=S[:, u % 2, h, :], scalar=theta[:, h:h + 1],
                                           in1=E[:, h, :], op0=ALU.is_ge, op1=ALU.mult).then_inc(s["late_prob"], 1)
                dve.wait_ge(s["late_prob"], HU * u + (g + 1) * REP)

            def norm_stats(q):
                tts = slice(PASSES[q][0], PASSES[q][-1] + 1)
                va, rs, t = var[:, tts], rstd[:, tts], sq[:, tts]
                pair(*[lambda tt=tt: v.bn_stats(st6[:, tt, :], r1[:, tt, :]) for tt in PASSES[q]])
                pair(*[lambda tt=tt: v.bn_aggr(mv[:, tt, :], st6[:, tt, :]) for tt in PASSES[q]])
                done(v.tensor_scalar(va, mv[:, tts, 1], EPS, None, ALU.add))
                done(v.tensor_scalar(rs.bitcast(I32), va.bitcast(I32), -0.5, RSQRT_BITS, ALU.mult, ALU.add))
                for _ in range(3):
                    done(v.tensor_tensor(t, rs, rs, ALU.mult))
                    done(v.scalar_tensor_tensor(out=t, in0=t, scalar=-0.5, in1=va, op0=ALU.mult, op1=ALU.mult))
                    done(v.scalar_tensor_tensor(out=rs, in0=t, scalar=1.5, in1=rs, op0=ALU.add, op1=ALU.mult))

            def normed(q, i):
                tt = PASSES[q][i]
                return v.tensor_scalar(x1[:, tt, :], r1[:, tt, :], mv[:, tt, 0:1], rstd[:, tt:tt + 1],
                                       ALU.subtract, ALU.mult)

            def out_add(q, i):
                tt = PASSES[q][i]
                if tt == 0:
                    dve.wait_ge(s["in_tok"], 32)
                dve.wait_ge(s["out_ready"], tt + 1)
                done(v.tensor_tensor(r1[:, tt, :], product_bank[tt][:], x_sb[:, tt, :], ALU.add))

            def first_norm(q):
                norm_stats(q)
                pair(*[lambda i=i: normed(q, i) for i in range(len(PASSES[q]))])

            def quantise(q, i):
                tt = PASSES[q][i]
                r = r1[:, tt, :]
                done(v.tensor_scalar(r, x1[:, tt, :], inv[:, 0:1], sc[:, 1:2], ALU.mult, ALU.add))
                done(v.tensor_scalar(r, r, 0.0, QMAX, ALU.max, ALU.min))
                done(v.tensor_scalar(r, r, MAGIC, None, ALU.add))
                signal(v.tensor_scalar(aq[:, tt, :], r, -(MAGIC + QMID), None, ALU.add, ALU.add,
                                       accum_out=arow[:, tt:tt + 1]), "quant_ready", tt + 1)
                done(v.tensor_scalar(arow[:, tt:tt + 1], arow[:, tt:tt + 1], zc[:, 1:2], None, ALU.mult))

            def cross_add(q, i):
                tt = PASSES[q][i]
                dve.wait_ge(s["cadd_ready"], B)
                dve.wait_ge(s["cross_ready"], tt + 1)
                done(v.scalar_tensor_tensor(out=r1[:, tt, :], in0=product_bank[tt][:], scalar=arow[:, tt:tt + 1],
                                            in1=cadd[:, tt // QT, :], op0=ALU.add, op1=ALU.add))
                done(v.scalar_tensor_tensor(out=r1[:, tt, :], in0=r1[:, tt, :], scalar=zc[:, 3:4],
                                            in1=x1[:, tt, :], op0=ALU.mult, op1=ALU.add))

            def second_norm(q):
                norm_stats(q)
                for i in range(len(PASSES[q])):
                    normed(q, i).then_inc(s["norm_ready"], 1)
                dve.wait_ge(s["norm_ready"], PASSES[q][-1] + 1)

            def gated(q, f):
                n, toks, w = q * NF + f, len(PASSES[q]) * P, TILES[q][f]
                gate, up = gate_up(q, f)
                g = g_sb[:, f % 2, 0:toks]
                dve.wait_ge(s["gate_done"], n + 1)
                done(v.scalar_tensor_tensor(out=g, in0=g, scalar=1.0, in1=gate, op0=ALU.add, op1=ALU.mult))
                signal(v.scalar_tensor_tensor(out=hT[:, f, 0:toks], in0=g, scalar=both_half[:, w:w + 1],
                                              in1=up, op0=ALU.mult, op1=ALU.mult), "h_ready", n + 1)

            def take_down(q):
                dve.wait_ge(s["ff_used"], NF * (q + 1))
                for tt in PASSES[q]:
                    v.tensor_tensor(r1[:, tt, :], turn_bank[tt][:], ds[:], ALU.mult).then_inc(s["down_used"], 1)
                dve.wait_ge(s["down_used"], PASSES[q][-1] + 1)

            def final_add(q, i):
                tt = PASSES[q][i]
                done(v.tensor_tensor(r1[:, tt, :], r1[:, tt, :], x1[:, tt, :], ALU.add))

            def final_norm(q, i):
                signal(normed(q, i), "y_ready", PASSES[q][i] + 1)

            dve.wait_ge(s["in_cst"], 48)
            signal(v.tensor_copy(identb[:], cst[:, 0:P]), "cst_ready", 1)
            signal(v.tensor_copy(causal[:], cst[:, P:2 * P]), "cst_ready", 2)
            signal(v.memset(onesb[:], 1.0), "cst_ready", 3)
            signal(v.memset(onesf[:], 1.0), "cst_ready", 4)
            done(v.memset(vaug[:], 1.0))
            done(v.reciprocal(inv[:], sc[:]))
            done(v.tensor_scalar(zc[:, 0:1], sc[:, 1:2], QMID, -1.0, ALU.subtract, ALU.mult))
            done(v.tensor_scalar(zc[:, 1:2], sc[:, 3:4], QMID, -1.0, ALU.subtract, ALU.mult))
            done(v.tensor_tensor(zc[:, 2:3], zc[:, 0:1], zc[:, 1:2], ALU.mult))
            done(v.tensor_scalar(zc[:, 2:3], zc[:, 2:3], float(D), None, ALU.mult))
            signal(v.tensor_tensor(zc[:, 3:4], sc[:, 0:1], sc[:, 2:3], ALU.mult), "scale_ready", 1)
            dve.wait_ge(s["in_gus"], 16)
            done(v.tensor_scalar(gate_half[:], gus_sb[:, 0, :], 0.5, None, ALU.mult))
            done(v.tensor_tensor(both_half[:], gate_half[:], gus_sb[:, 1, :], ALU.mult))
            walk({"rotate": project, "take": take, "early_norm": early_norm, "guess": guess, "adjust": adjust,
                  "aim": aim, "eight": eight, "pick": pick, "keep": keep, "keep_group": keep_group, "late_norm": late_norm,
                  "out_add": out_add, "first_norm": first_norm, "quantise": quantise, "cross_add": cross_add,
                  "second_norm": second_norm, "gated": gated, "take_down": take_down,
                  "final_add": final_add, "final_stats": norm_stats, "final_norm": final_norm})



def normal_quantile(p):
    lo, hi = -8.0, 8.0
    for _ in range(60):
        mid = (lo + hi) / 2
        lo, hi = (mid, hi) if (1 + math.erf(mid / math.sqrt(2))) / 2 < p else (lo, mid)
    return (lo + hi) / 2


def kernel(**inputs):
    import concourse.bacc as bacc
    from concourse.bass_utils import run_bass_kernel_spmd

    a = {k: np.asarray(v) for k, v in inputs.items()}

    freq = 1.0 / np.float32(THETA) ** (np.arange(0, HD, 2, dtype=np.float32) / np.float32(HD))
    ang = np.outer(np.arange(SEQ, dtype=np.float32), freq).astype(np.float32)
    ang = np.concatenate([ang, ang], axis=-1)
    sign = np.concatenate([-np.ones(HD // 2), np.ones(HD // 2)]).astype(np.float32)
    table = np.stack([np.cos(ang), np.sin(ang) * sign], axis=1).astype(np.float32)
    rope = np.stack([table * np.float32(SHRINK), table], axis=1)
    causal = np.triu(np.full((P, P), MASKED, np.float32), 1)
    seen = [P + 1 + r for r in range(P)]
    z = [normal_quantile(1 - KEEP / n) for n in seen]
    z_neg = np.array([[-q] for q in z], np.float32)
    k_unit = np.array([[BOLD / (2 * n * math.exp(-q * q / 2) / math.sqrt(2 * math.pi))] for n, q in zip(seen, z)],
                      np.float32)
    places = np.broadcast_to(np.arange(8, dtype=np.float32) + np.float32(0.5), (P, 8))
    consts = np.concatenate([np.eye(P, dtype=np.float32), causal, z_neg, k_unit, places,
                             np.zeros((P, 6), np.float32)], axis=1)

    def hidden_columns(w):
        padded = np.zeros((NF * P, D), w.dtype)
        padded[:DFF] = w
        return padded.reshape(NF, P, KD, P).transpose(0, 3, 2, 1).reshape(NF, P, D)

    down = np.zeros((NF * P, D), a["L0_ffn_down_w"].dtype)
    down[:DFF] = a["L0_ffn_down_w"].T
    ffw = np.concatenate([hidden_columns(a["L0_ffn_gate_w"]), hidden_columns(a["L0_ffn_up_w"]),
                          down.reshape(NF, P, D)], axis=2)
    gus = np.zeros((2, NF * P), np.float32)
    gus[0, :DFF], gus[1, :DFF] = a["L0_ffn_gate_s"], a["L0_ffn_up_s"]
    arrays = {
        "x": a["x"],
        "xT": a["x"].reshape(B * SEQ, D).T,
        "ctx": a["ctx_4096"],
        "wqkvT": np.concatenate([a["L0_attn_Wq"], a["L0_attn_Wk"], a["L0_attn_Wv"]], axis=0).T,
        "woT": a["L0_attn_Wo"].T,
        "scal": np.concatenate([a["L0_xattn_x1_scale"], a["L0_xattn_x1_zp"],
                                a["L0_xattn_x2_scale"], a["L0_xattn_x2_zp"]]),
        "ffw": ffw,
        "gus": gus.reshape(2, NF, P).transpose(2, 0, 1),
        "down_s": a["L0_ffn_down_s"],
        "rope": rope,
        "consts": consts,
    }
    arrays = {k: np.ascontiguousarray(w) for k, w in arrays.items()}
    nc = bacc.Bacc("TRN2", target_bir_lowering=False, num_devices=1)
    args = [nc.dram_tensor(k, w.shape, mybir.dt.from_np(w.dtype), kind="ExternalInput").ap() for k, w in arrays.items()]
    out = nc.dram_tensor("out", (B, SEQ, D), F32, kind="ExternalOutput").ap()
    decoder_layer(nc, *args, out)
    result = run_bass_kernel_spmd(nc, [arrays], core_ids=[0])
    return result.results[0]["out"]
```
